# Optimizing a Trainium2 kernel written in Bass

```python
import numpy as np
import jax
import jax.numpy as jnp

def _softmax(x, axis=-1):
    return jax.nn.softmax(x, axis=axis)

def _gelu(x):
    return jax.nn.gelu(x, approximate=True)

def _silu(x):
    return jax.nn.silu(x)

def _sigmoid(x):
    return jax.nn.sigmoid(x)

def _layernorm(x, axis=-1, eps=1e-05):
    m = jnp.mean(x, axis=axis, keepdims=True)
    v = jnp.var(x, axis=axis, keepdims=True)
    return (x - m) / jnp.sqrt(v + eps)

def _scatter_add(tgt, idx, src, axis=0):
    return tgt.at[idx].add(src)

def _segment_sum(src, seg, n):
    return jax.ops.segment_sum(src, seg, n)
kernel_name = 'mk_seq_preln_d1_jaxref_r4_02b838'

def setup_inputs(seed: int=0):
    np.random.seed(seed)
    _w = jnp.asarray

    def _L0_attn_setup():
        import jax, jax.numpy as jnp
        import numpy as np
        NUM_HEADS = 16
        key = jax.random.key(seed)
        ks = jax.random.split(key, 4)
        B, S, D = (2, 512, 256)
        x = jax.random.normal(ks[0], (B, S, D), dtype=jnp.float32)
        W_exp = jax.random.normal(ks[1], (D, 3 * D), dtype=jnp.float32) * (1.0 / np.sqrt(D))
        b_exp = jnp.zeros((3 * D,), dtype=jnp.float32)
        W_comp = jax.random.normal(ks[2], (D, D), dtype=jnp.float32) * (1.0 / np.sqrt(D))
        b_comp = jnp.zeros((D,), dtype=jnp.float32)
        return {'x': x, 'W_exp': W_exp, 'b_exp': b_exp, 'W_comp': W_comp, 'b_comp': b_comp}
    _L0_attn_in = _L0_attn_setup()

    def _L0_ffn_setup():
        import jax, jax.numpy as jnp
        import numpy as np
        DIM = 256
        HIDDEN = 768
        SCALE = 1.0 / 127.0

        def _dequant(w_int, dtype):
            return w_int.astype(dtype) * jnp.asarray(SCALE, dtype)
        key = jax.random.key(seed)
        k_x, k_g, k_u, k_d = jax.random.split(key, 4)
        x = jax.random.normal(k_x, (4, 512, DIM), dtype=jnp.float32)
        w_gate = jax.random.randint(k_g, (HIDDEN, DIM), -127, 128, dtype=jnp.int32)
        w_up = jax.random.randint(k_u, (HIDDEN, DIM), -127, 128, dtype=jnp.int32)
        w_down = jax.random.randint(k_d, (DIM, HIDDEN), -127, 128, dtype=jnp.int32)
        return {'x': x, 'w_gate': w_gate, 'w_up': w_up, 'w_down': w_down}
    _L0_ffn_in = _L0_ffn_setup()
    _d = {'L0_attn_x': _L0_attn_in['x'], 'L0_attn_W_exp': _L0_attn_in['W_exp'], 'L0_attn_b_exp': _L0_attn_in['b_exp'], 'L0_attn_W_comp': _L0_attn_in['W_comp'], 'L0_attn_b_comp': _L0_attn_in['b_comp'], 'L0_ffn_w_gate': _L0_ffn_in['w_gate'], 'L0_ffn_w_up': _L0_ffn_in['w_up'], 'L0_ffn_w_down': _L0_ffn_in['w_down']}
    _x0 = _d['L0_attn_x']
    _d['L0_attn_x'] = jax.random.normal(jax.random.fold_in(jax.random.key(seed), 1), (2, 2048, 256), dtype=_x0.dtype)
    del _x0
    return _d

def reference(L0_attn_x, L0_attn_W_exp, L0_attn_b_exp, L0_attn_W_comp, L0_attn_b_comp, L0_ffn_w_gate, L0_ffn_w_up, L0_ffn_w_down):

    def _L0_attn_ref(x, W_exp, b_exp, W_comp, b_comp):
        import jax, jax.numpy as jnp
        import numpy as np
        NUM_HEADS = 16
        B, S, D = x.shape
        H = NUM_HEADS
        hd = D // H
        qkv = jnp.einsum('bsd,de->bse', x, W_exp) + b_exp
        q, k, v = jnp.split(qkv, 3, axis=-1)

        def split_heads(t):
            return t.reshape(B, S, H, hd).transpose(0, 2, 1, 3)
        q, k, v = (split_heads(q), split_heads(k), split_heads(v))
        scores = jnp.einsum('bhqd,bhkd->bhqk', q, k) * jax.lax.rsqrt(jnp.float32(hd))
        mask = (jnp.arange(S)[:, None] >= jnp.arange(S)[None, :]).astype(jnp.float32)
        scores = scores * mask - 10000000000.0 * (1.0 - mask)
        attn = jax.nn.softmax(scores, axis=-1)
        ctx = jnp.einsum('bhqk,bhkd->bhqd', attn, v)
        ctx = ctx.transpose(0, 2, 1, 3).reshape(B, S, D)
        out = jnp.einsum('bsd,de->bse', ctx, W_comp) + b_comp
        return out

    def _L0_ffn_ref(x, w_gate, w_up, w_down):
        import jax, jax.numpy as jnp
        import numpy as np
        DIM = 256
        HIDDEN = 768
        SCALE = 1.0 / 127.0

        def _dequant(w_int, dtype):
            return w_int.astype(dtype) * jnp.asarray(SCALE, dtype)
        wg = _dequant(w_gate, x.dtype)
        wu = _dequant(w_up, x.dtype)
        wd = _dequant(w_down, x.dtype)
        gate = jnp.einsum('bsd,hd->bsh', x, wg)
        up = jnp.einsum('bsd,hd->bsh', x, wu)
        h = jax.nn.silu(gate) * up
        return jnp.einsum('bsh,dh->bsd', h, wd)
    x = L0_attn_x
    x = x + _L0_attn_ref(_layernorm(x, axis=-1), L0_attn_W_exp, L0_attn_b_exp, L0_attn_W_comp, L0_attn_b_comp)
    x = x + _L0_ffn_ref(_layernorm(x, axis=-1), L0_ffn_w_gate, L0_ffn_w_up, L0_ffn_w_down)
    return x

_drawn_inputs = setup_inputs


def setup_inputs(seed=0):
    import zlib

    import numpy as np

    out = dict(_drawn_inputs(seed))
    spreads = {'L0_attn_b_exp': (0.0, 0.1), 'L0_attn_b_comp': (0.0, 0.1)}
    factors = {}
    for name, (base, spread) in spreads.items():
        noise = np.random.default_rng([zlib.crc32(name.encode()), seed]).standard_normal(out[name].shape)
        drawn = base * np.exp(spread * noise) if base else spread * noise
        out[name] = jnp.asarray(drawn.astype(out[name].dtype))
    for name, factor in factors.items():
        out[name] = (out[name] * factor).astype(out[name].dtype)
    return out
```

```python
import concourse.bass as bass
from concourse import mybir
from contextlib import ExitStack

F32 = mybir.dt.float32
F32R = mybir.dt.float32r
I32 = mybir.dt.int32
ALU = mybir.AluOpType
ACT = mybir.ActivationFunctionType
AX = mybir.AxisListType

P = 128
B, S, D = 2, 2048, 256
H = 16
HD = D // H
TOK = B * S
FH = 768
EPS = 1e-5
SCALE = HD ** -0.5
W_SCALE = 1.0 / 127.0

CH = 512
NCH = TOK // CH
CT = CH // P
KD = D // P
QKT = 2 * D // P
MF = FH // P

QC = S // CH
KT = S // P
UH = 4
UG = H // UH
PAIRS = UH // 2
HALF = 3 * HD
ROWS = PAIRS * HALF
ROWSM = ROWS + 2
VW = 32
JU = sum(CT * (c + 1) for c in range(QC))
PRING = 8
RING = 3
NEG = -3.0e38
FREE = 1


def sbuf(nc, ctx, name, shape, dt=F32):
    return ctx.enter_context(nc.sbuf_tensor(name, shape, dt))


def wait_apart(eng, sem, count, passed):
    eng.wait_ge(sem, count)
    if not isinstance(count, int):
        eng.sem_inc(passed, 1)


def banks(nc, ctx, name, n):
    return [ctx.enter_context(nc.psum_tensor(f"{name}{i}", [P, CH], F32)) for i in range(n)]


def project(nc, x, w_exp, b_exp, qk_scratch, v_scratch, ident, minus_half):
    with ExitStack() as ctx:
        def sem(name):
            return ctx.enter_context(nc.semaphore(name))

        w = sbuf(nc, ctx, "w", [P, KD, 3 * D])
        w_hi = sbuf(nc, ctx, "w_hi", [P, KD, 3 * D], F32R)
        w_lo = sbuf(nc, ctx, "w_lo", [P, KD, 3 * D], F32R)
        bqk = sbuf(nc, ctx, "bqk", [P, QKT])
        bv = sbuf(nc, ctx, "bv", [P, D])
        xt = sbuf(nc, ctx, "xt", [P, CT, D])
        xn = sbuf(nc, ctx, "xn", [P, CT, D])
        stats = sbuf(nc, ctx, "stats", [P, CT, 6])
        meanvar = sbuf(nc, ctx, "meanvar", [P, CT, 2])
        var_eps = sbuf(nc, ctx, "var_eps", [P, CT])
        rstd = sbuf(nc, ctx, "rstd", [P, CT])
        xT_hi = sbuf(nc, ctx, "xT_hi", [P, KD, CH], F32R)
        xT_lo = sbuf(nc, ctx, "xT_lo", [P, KD, CH], F32R)
        qk_hi = sbuf(nc, ctx, "qk_hi", [P, QKT, CH], F32R)
        qk_lo = sbuf(nc, ctx, "qk_lo", [P, QKT, CH], F32R)
        vs = sbuf(nc, ctx, "vs", [P, CT, D])
        t_ps = banks(nc, ctx, "xT_ps", KD)
        qk_ps = banks(nc, ctx, "qk_ps", QKT)
        v_ps = banks(nc, ctx, "v_ps", 2)

        w_in, b_in, x_in = sem("w_in"), sem("b_in"), sem("x_in")
        ident_set, ident_made, exponent_set = sem("ident_set"), sem("ident_made"), sem("exponent_set")
        w_hi_done, w_lo_done = sem("w_hi_done"), sem("w_lo_done")
        stats_done, aggr_done, rstd_done, normed = sem("stats_done"), sem("aggr_done"), sem("rstd_done"), sem("normed")
        eps_added, passed = sem("eps_added"), sem("passed")
        turned, xT_hi_done, xT_lo_done = sem("turned"), sem("xT_hi_done"), sem("xT_lo_done")
        qk_full, qk_hi_done, qk_lo_done = sem("qk_full"), sem("qk_hi_done"), sem("qk_lo_done")
        qk_stored = [sem(f"qk_stored{m}") for m in range(QKT)]
        v_full, v_done, v_stored = sem("v_full"), sem("v_done"), sem("v_stored")

        block = ctx.enter_context(nc.Block())

        @block.sync
        def _(sp):
            def load_x(n):
                sp.dma_start(xt[:], x[bass.ds(n * CH, CH), :].rearrange("(t p) d -> p t d", p=P)).then_inc(x_in, 16)

            def store(n):
                for m in range(QKT):
                    sp.wait_ge(qk_lo_done, n * QKT + m + 1)
                    for part, half in enumerate((qk_hi, qk_lo)):
                        sp.dma_start(qk_scratch[part, m * P:(m + 1) * P, bass.ds(n * CH, CH)],
                                     half[:, m, :].bitcast(F32)).then_inc(qk_stored[m], 16)
                sp.wait_ge(v_done, n * 2 + 2)
                sp.dma_start(v_scratch[bass.ds(n * CH, CH), :].rearrange("(t p) d -> p t d", p=P),
                             vs[:]).then_inc(v_stored, 16)

            for m in range(QKT):
                sp.sem_inc(qk_stored[m], FREE)
            sp.sem_inc(v_stored, FREE)
            load_x(0)
            sp.dma_start(w[:], w_exp.rearrange("(k p) n -> p k n", p=P)).then_inc(w_in, 16)
            sp.dma_start(bqk[:], b_exp[0:2 * D].rearrange("(m p) -> p m", p=P),
                         allow_slow_non_contiguous=True).then_inc(b_in, 16)
            sp.dma_start(bv[:], b_exp[2 * D:3 * D].rearrange("(a d) -> a d", a=1).to_broadcast([P, D])).then_inc(b_in, 16)
            sp.wait_ge(normed, CT)
            load_x(1)
            with sp.Fori(0, NCH - 2) as n:
                sp.wait_ge(normed, (n + 2) * CT)
                load_x(n + 2)
                store(n)
            store(NCH - 2)
            store(NCH - 1)
            for m in range(QKT):
                sp.wait_ge(qk_stored[m], NCH * 32 + FREE)
            sp.wait_ge(v_stored, NCH * 16 + FREE)

        @block.gpsimd
        def _(pool):
            pool.memset(ident[:], 0.0).then_inc(ident_set, 1)
            pool.wait_ge(ident_set, 1)
            pool.affine_select(out=ident[:], in_=ident[:], compare_op=ALU.not_equal, fill=1.0, base=0,
                               pattern=[[-1, P]], channel_multiplier=1).then_inc(ident_made, 1)

            def inverse_deviation(n):
                wait_apart(pool, aggr_done, n * CT + CT, passed)
                pool.tensor_scalar(var_eps[:], meanvar[:, :, 1], EPS, None, ALU.add).then_inc(eps_added, 1)
                pool.wait_ge(eps_added, n + 1)
                pool.tensor_tensor(rstd[:], var_eps[:], minus_half[:], ALU.pow).then_inc(rstd_done, 1)

            pool.memset(minus_half[:], -0.5).then_inc(exponent_set, 1)
            pool.wait_ge(exponent_set, 1)
            with pool.Fori(0, NCH) as n:
                inverse_deviation(n)

        @block.scalar
        def _(act):
            def xT_high(n):
                for k in range(KD):
                    act.wait_ge(turned, n * KD + k + 1)
                    act.activation(xT_hi[:, k, :], t_ps[k][:], ACT.Copy).then_inc(xT_hi_done, 1)

            def qk_high(n):
                for m in range(QKT):
                    act.wait_ge(qk_full, n * QKT + m + 1)
                    act.wait_ge(qk_stored[m], n * 32 + FREE)
                    act.activation(qk_hi[:, m, :], qk_ps[m][:], ACT.Identity, bias=bqk[:, m:m + 1]
                                   ).then_inc(qk_hi_done, 1)

            act.wait_ge(w_in, 16)
            act.activation(w_hi[:], w[:], ACT.Copy).then_inc(w_hi_done, 1)
            act.wait_ge(b_in, 32)
            xT_high(0)
            with act.Fori(0, NCH - 1) as n:
                qk_high(n)
                xT_high(n + 1)
            qk_high(NCH - 1)

        @block.vector
        def _(dve):
            def norm(n):
                dve.wait_ge(x_in, n * 16 + 16)
                for t in range(CT):
                    dve.bn_stats(stats[:, t, :], xt[:, t, :]).then_inc(stats_done, 1)
                for t in range(CT):
                    wait_apart(dve, stats_done, n * CT + t + 1, passed)
                    dve.bn_aggr(meanvar[:, t, :], stats[:, t, :]).then_inc(aggr_done, 1)
                dve.wait_ge(rstd_done, n + 1)
                for t in range(CT):
                    dve.tensor_scalar(xn[:, t, :], xt[:, t, :], meanvar[:, t, 0:1], rstd[:, t:t + 1],
                                      ALU.subtract, ALU.mult).then_inc(normed, 1)

            def xT_low(n):
                for k in range(KD):
                    dve.wait_ge(xT_hi_done, n * KD + k + 1)
                    dve.tensor_tensor(xT_lo[:, k, :], t_ps[k][:], xT_hi[:, k, :].bitcast(F32), ALU.subtract).then_inc(xT_lo_done, 1)

            def qkv_low(n):
                for m in range(QKT):
                    dve.wait_ge(qk_hi_done, n * QKT + m + 1)
                    dve.scalar_tensor_tensor(out=qk_lo[:, m, :], in0=qk_ps[m][:], scalar=bqk[:, m:m + 1],
                                             in1=qk_hi[:, m, :].bitcast(F32), op0=ALU.add, op1=ALU.subtract).then_inc(qk_lo_done, 1)
                dve.wait_ge(v_stored, n * 16 + FREE)
                for i in range(2):
                    dve.wait_ge(v_full, n * 2 + i + 1)
                    dve.tensor_tensor(vs[:, 2 * i:2 * i + 2, :], v_ps[i][:].rearrange("p (t d) -> p t d", d=D),
                                      bv[:, None, :].to_broadcast([P, 2, D]), ALU.add).then_inc(v_done, 1)

            norm(0)
            dve.wait_ge(w_hi_done, 1)
            dve.tensor_tensor(w_lo[:], w[:], w_hi[:].bitcast(F32), ALU.subtract).then_inc(w_lo_done, 1)
            dve.wait_ge(b_in, 32)
            xT_low(0)
            with dve.Fori(0, NCH - 1) as n:
                norm(n + 1)
                qkv_low(n)
                xT_low(n + 1)
            qkv_low(NCH - 1)

        @block.tensor
        def _(pe):
            def turn(n):
                pe.wait_ge(normed, n * CT + CT)
                for k in range(KD):
                    for t in range(CT):
                        mm = pe.transpose(t_ps[k][:, t * P:(t + 1) * P], xn[:, t, k * P:(k + 1) * P], ident[:])
                    mm.then_inc(turned, 1)

            terms = [(w_hi, xT_hi), (w_lo, xT_hi), (w_hi, xT_lo)]

            def project_chunk(n):
                pe.wait_ge(xT_lo_done, n * KD + KD)
                for m in range(QKT):
                    for i, (k, (wx, xx)) in enumerate([(k, t) for k in range(KD) for t in terms]):
                        mm = pe.matmul(qk_ps[m][:], wx[:, k, m * P:(m + 1) * P], xx[:, k, :],
                                       start=(i == 0), stop=(i == 3 * KD - 1))
                    mm.then_inc(qk_full, 1)
                for t in range(CT):
                    for i, (k, (wx, xx)) in enumerate([(k, t_) for k in range(KD) for t_ in terms]):
                        mm = pe.matmul(v_ps[t // 2][:, (t % 2) * D:(t % 2 + 1) * D], xx[:, k, t * P:(t + 1) * P],
                                       wx[:, k, 2 * D:3 * D], start=(i == 0), stop=(i == 3 * KD - 1))
                    if t % 2:
                        mm.then_inc(v_full, 1)

            pe.wait_ge(ident_made, 1)
            turn(0)
            pe.wait_ge(w_lo_done, 1)
            with pe.Fori(0, NCH - 1) as n:
                project_chunk(n)
                turn(n + 1)
            project_chunk(NCH - 1)


def ring_events(with_max, with_ctx):
    events = []
    for c in range(QC):
        scores = [("scores", c, t, h, i) for t in range(CT) for h in range(UH) for i in range(c + 1)]
        for j in range(CT * (c + 1)):
            if with_max:
                events.append([scores.pop(0) for _ in range(UH)])
            else:
                events.append([])
            if c and j == 1 and with_max:
                events[-1].append(("max_rows", c - 1))
            if c and j == 2 and with_ctx:
                events[-1].append(("ctx_rows", c - 1))
    last = ([("max_rows", QC - 1)] if with_max else []) + ([("ctx_rows", QC - 1)] if with_ctx else [])
    return events + [last]


def attend(nc, qk_scratch, v_scratch, ctx_all, ident):
    with ExitStack() as ctx:
        def sem(name):
            return ctx.enter_context(nc.semaphore(name))

        q_sb = [sbuf(nc, ctx, f"q_sb{b}", [P, UH, S], F32R) for b in range(B)]
        k_sb = [sbuf(nc, ctx, f"k_sb{b}", [P, PAIRS, S], F32R) for b in range(B)]
        v_sb = [sbuf(nc, ctx, f"v_sb{b}", [P, KT, UH, VW]) for b in range(B)]
        probs = sbuf(nc, ctx, "probs", [P, PRING, 2, CH])
        mask = sbuf(nc, ctx, "mask", [P, CH])
        unread = sbuf(nc, ctx, "unread", [P, RING, CH])
        part_max = sbuf(nc, ctx, "part_max", [P, 2, CT * UH, QC])
        row_max = sbuf(nc, ctx, "row_max", [P, 2, CT * UH])
        neg_max = sbuf(nc, ctx, "neg_max", [P, 2, CT * UH, 2])
        max_rows = sbuf(nc, ctx, "max_rows", [2 * UH, 2, CH], F32R)
        ctxT = sbuf(nc, ctx, "ctxT", [P, 2, CH])
        inv_sum = sbuf(nc, ctx, "inv_sum", [P, 2, CT, UH])
        ring = banks(nc, ctx, "ring", RING)
        score_ps = [ctx.enter_context(nc.psum_tensor(f"score_ps{p}", [P, 2, CH], F32)) for p in range(PAIRS)]
        out_ps = banks(nc, ctx, "out_ps", 1)[0]

        q_zero, ones_set, v_ones_set, mask_zero, mask_made = sem("q_zero"), sem("ones_set"), sem("v_ones_set"), sem("mask_zero"), sem("mask_made")
        v_zero, passed = sem("v_zero"), sem("passed1")
        loaded = [[sem(f"loaded{b}_{c}") for c in range(QC)] for b in range(B)]
        ring_full, ring_free = sem("ring_full"), sem("ring_free")
        max_done, max_hi_done, max_split = sem("max_done"), sem("max_hi_done"), sem("max_split")
        max_loaded = [sem(f"max_loaded{i}") for i in range(2)]
        scores_full, probs_done, probs_masked = sem("scores_full"), sem("probs_done"), sem("probs_masked")
        pv_done, out_copied, inv_done = sem("pv_done"), sem("out_copied"), sem("inv_done")

        first_len = sum(len(e) for e in ring_events(True, False))
        step_len = sum(len(e) for e in ring_events(True, True))
        assert step_len % RING == 0
        NDIAG = QC * CT * PAIRS
        before = [sum(CT * (a + 1) for a in range(c)) for c in range(QC + 1)]

        def index_of(events, event):
            return [e for es in events for e in es].index(event)

        full_step = ring_events(True, True)
        SC, PC = PAIRS, PRING // PAIRS

        def all_steps(eng, step):
            with eng.Fori(0, UG - 1) as i:
                step(i, 0, True)
                step(i, 1, True)
            step(UG - 1, 0, True)
            step(UG - 1, 1, False)

        block = ctx.enter_context(nc.Block())

        @block.sync
        def _(sp):
            def load(g, b, c):
                toks = slice(b * S + c * CH, b * S + (c + 1) * CH)
                for dst, first, parts in ((q_sb[b], 0, (0, 0, 1)), (k_sb[b], D, (0, 1, 0))):
                    for r, part in enumerate(parts):
                        rows = qk_scratch[part, bass.ds(g * (UH * HD) + first, UH * HD), toks]
                        rows = rows.rearrange("(pair e r) t -> e r pair t", e=2, r=HD)
                        for e in range(2):
                            at = HALF * e + HD * r
                            to = dst[at:at + HD, e:UH:2, c * CH:(c + 1) * CH] if first == 0 else dst[at:at + HD, :, c * CH:(c + 1) * CH]
                            sp.dma_start(to.bitcast(F32), rows[e]).then_inc(loaded[b][c], 16)
                for t in range(c * CT, (c + 1) * CT):
                    v = v_scratch[b * S + t * P:b * S + (t + 1) * P, bass.ds(g * (UH * HD), UH * HD)]
                    sp.dma_start(v_sb[b][:, t, :, 0:HD], v.rearrange("p (h d) -> p h d", h=UH)
                                 ).then_inc(loaded[b][c], 16)

            def place_max(b, c, at):
                sp.wait_ge(ring_free, at)
                for h in range(UH):
                    sp.dma_start(q_sb[b][ROWS:ROWSM, h, c * CH:(c + 1) * CH].bitcast(F32),
                                 max_rows[2 * h:2 * h + 2, c % 2, :].bitcast(F32)).then_inc(max_loaded[c % 2], 16)

            def step(i, b, more):
                s = i * 2 + b
                base = s * step_len + first_len
                for c in range(QC):
                    if more:
                        place_max(1 - b, c, base + index_of(full_step, ("max_rows", c)) + 1)
                    if c == QC - 2 and not isinstance(i, int):
                        for x in range(QC - 1):
                            sp.wait_ge(pv_done, s * JU + (before[QC - 1] + CT * (x + 1)) + PC)
                            load(i + 1, b, x)
                if not isinstance(i, int):
                    sp.wait_ge(pv_done, s * JU + (JU + PC))
                    load(i + 1, b, QC - 1)

            sp.wait_ge(q_zero, B)
            sp.wait_ge(ones_set, B)
            sp.wait_ge(v_ones_set, B)
            for b in range(B):
                for c in range(QC):
                    load(0, b, c)
            first = ring_events(True, False)
            for c in range(QC):
                place_max(0, c, index_of(first, ("max_rows", c)) + 1)
            all_steps(sp, step)

        @block.gpsimd
        def _(pool):
            for b in range(B):
                pool.memset(q_sb[b][0:ROWS].bitcast(F32), 0.0).then_inc(q_zero, 1)
                pool.wait_ge(q_zero, b + 1)
                pool.memset(k_sb[b][ROWS:ROWSM].bitcast(F32), 1.0).then_inc(ones_set, 1)
                pool.wait_ge(ones_set, b + 1)
            for b in range(B):
                pool.memset(v_sb[b][:], 0.0).then_inc(v_zero, 1)
                pool.wait_ge(v_zero, b + 1)
                pool.memset(v_sb[b][:, :, :, HD:HD + 1], 1.0).then_inc(v_ones_set, 1)
            pool.memset(mask[:], 0.0).then_inc(mask_zero, 1)
            pool.wait_ge(mask_zero, 1)
            pool.affine_select(out=mask[:, CH - P:CH], in_=mask[:, CH - P:CH], compare_op=ALU.is_ge, fill=NEG,
                               base=0, pattern=[[-1, P]], channel_multiplier=1).then_inc(mask_made, 1)

            def step(i, b, more):
                s = i * 2 + b
                for c in range(QC):
                    for r in range(CT):
                        j = before[c] + CT * c + r
                        for pair in range(PAIRS):
                            n = PAIRS * j + pair
                            wait_apart(pool, probs_done, s * (PAIRS * JU) + (n + 1 + SC), passed)
                            at = probs[:, n % PRING, :, P * r:P * (r + 1)]
                            pool.affine_select(out=at, in_=at, compare_op=ALU.is_ge, fill=0.0, base=0,
                                               pattern=[[0, 2], [1, P]], channel_multiplier=-1).then_inc(probs_masked, 1)

            all_steps(pool, step)

        @block.scalar
        def _(act):
            act.sem_inc(probs_done, SC)
            act.sem_inc(out_copied, FREE)

            def copy_out(i, b, c):
                s = i * 2 + b
                act.wait_ge(pv_done, s * JU + (before[c + 1] + PC))
                if c >= 2:
                    last = ("ctx_rows", c - 2)
                    if isinstance(i, int) and b == 1:
                        act.wait_ge(ring_full, (2 * UG - 1) * step_len + first_len + c - 1)
                    else:
                        act.wait_ge(ring_full, s * step_len + (first_len + index_of(full_step, last) + 1))
                else:
                    back = first_len - step_len + index_of(full_step, ("ctx_rows", c + 2)) + 1
                    act.wait_ge(ring_full, s * step_len + back)
                act.activation(ctxT[:, c % 2, :], out_ps[:], ACT.Copy).then_inc(out_copied, 1)

            def step(i, b, more):
                s = i * 2 + b
                for c in range(QC):
                    for jj in range(CT * (c + 1)):
                        j = before[c] + jj
                        lo = P * max(0, jj - CT * c)
                        for pair in range(PAIRS):
                            n = PAIRS * j + pair
                            act.wait_ge(scores_full, s * (PAIRS * JU) + (n + 1))
                            if pair == 0:
                                act.wait_ge(pv_done, s * JU + (j + 1))
                            act.activation(probs[:, n % PRING, :, lo:CH], score_ps[pair][:, :, lo:CH], ACT.Exp,
                                           scale=SCALE).then_inc(probs_done, 1)
                        if c and jj == 0:
                            copy_out(i, b, c - 1)
                copy_out(i, b, QC - 1)

            all_steps(act, step)

        @block.vector
        def _(dve):
            def take(event, s, base, k, u_count):
                kind, c = event[0], event[1]
                bank = ring[k_of(k)]
                if kind == "scores" and event[4] == c:
                    wait_apart(dve, ring_full, base + (k + 1), passed)
                else:
                    dve.wait_ge(ring_full, base + (k + 1))
                if kind == "scores":
                    _, _, t, h, x = event
                    to = part_max[:, c % 2, t * UH + h, x:x + 1]
                    if x < c:
                        dve.tensor_reduce(to, bank[:], AX.X, ALU.max).then_inc(ring_free, 1)
                    else:
                        n = P * (t + 1)
                        dve.tensor_tensor_reduce(unread[:, k_of(k), 0:n], bank[:, 0:n], mask[:, CH - n:CH], 1.0, NEG,
                                                 ALU.add, ALU.max, to).then_inc(ring_free, 1)
                    if (t, h, x) == (CT - 1, UH - 1, c):
                        m = u_count(c)
                        dve.wait_ge(ring_free, base + (k + 1))
                        dve.tensor_reduce(row_max[:, c % 2, :], part_max[:, c % 2, :, 0:c + 1], AX.X, ALU.max
                                          ).then_inc(max_done, 1)
                        dve.wait_ge(max_done, m + 1)
                        dve.tensor_scalar(neg_max[:, c % 2, :, 0].bitcast(F32R), row_max[:, c % 2, :], -1.0, None, ALU.mult
                                          ).then_inc(max_hi_done, 1)
                        dve.wait_ge(max_hi_done, m + 1)
                        dve.scalar_tensor_tensor(out=neg_max[:, c % 2, :, 1], in0=row_max[:, c % 2, :], scalar=-1.0,
                                                 in1=neg_max[:, c % 2, :, 0], op0=ALU.mult, op1=ALU.subtract
                                                 ).then_inc(max_split, 1)
                elif kind == "max_rows":
                    m = u_count(c)
                    if not (isinstance(m, int) and m < 2):
                        dve.wait_ge(max_loaded[c % 2], (u_count(0) * 32) + 64 * (c // 2))
                    dve.tensor_copy(max_rows[:, c % 2, :], bank[0:2 * UH, :]).then_inc(ring_free, 1)
                else:
                    rows = bank[:].rearrange("p (t h w) -> p t h w", t=CT, h=UH)
                    dve.reciprocal(inv_sum[:, c % 2], rows[:, :, :, HD]).then_inc(inv_done, 1)
                    dve.wait_ge(inv_done, s * QC + (c + 1))
                    i, b = where[0]
                    for t in range(CT):
                        to = ctx_all[:, b * KT + c * CT + t, bass.ds(i * (UH * HD), UH * HD)].rearrange("p (h d) -> p h d", h=UH)
                        op = dve.tensor_tensor(to, rows[:, t, :, 0:HD],
                                               inv_sum[:, c % 2, t, :, None].to_broadcast([P, UH, HD]), ALU.mult)
                    op.then_inc(ring_free, 1)

            where = [None]
            shift = [0]

            def k_of(k):
                return (shift[0] + k) % RING

            def run(events, s, base, u_count):
                for k, event in enumerate(e for es in events for e in es):
                    take(event, s, base, k, u_count)

            dve.wait_ge(mask_made, 1)
            run(ring_events(True, False), None, 0, lambda c: c)
            shift[0] = first_len % RING

            def step(i, b, more):
                where[0] = (i, b)
                s = i * 2 + b
                base = s * step_len + first_len
                run(ring_events(more, True), s, base, lambda c: s * QC + (QC + c))

            all_steps(dve, step)

        @block.tensor
        def _(pe):
            pe.sem_inc(pv_done, PC)

            def fill(event, s, base, k, shift, b_max, max_count):
                kind, c = event[0], event[1]
                bank = ring[(shift + k) % RING]
                if not (isinstance(base, int) and base + k < RING):
                    pe.wait_ge(ring_free, base + (k - RING + 1))
                if kind == "scores":
                    _, _, t, h, x = event
                    q_at = c * CH + t * P
                    n = P * (t + 1) if x == c else CH
                    mm = pe.matmul(bank[:, 0:n], q_sb[b_max][0:ROWS, h, q_at:q_at + P],
                                   k_sb[b_max][0:ROWS, h // 2, x * CH:x * CH + n], start=True, stop=True)
                elif kind == "max_rows":
                    pe.wait_ge(max_split, max_count + (c + 1))
                    for t in range(CT):
                        mm = pe.transpose(bank[0:2 * UH, t * P:(t + 1) * P],
                                          neg_max[:, c % 2, t * UH:(t + 1) * UH, :].rearrange("p h x -> p (h x)"), ident[:])
                else:
                    pe.wait_ge(out_copied, s * QC + (c + 1 + FREE))
                    for t in range(CT):
                        mm = pe.transpose(bank[:, t * P:(t + 1) * P], ctxT[:, c % 2, t * P:(t + 1) * P], ident[:])
                mm.then_inc(ring_full, 1)

            def scores(s, b, c, jj, pair):
                n = PAIRS * (before[c] + jj) + pair
                lo = P * max(0, jj - CT * c)
                pe.wait_ge(probs_done, s * (PAIRS * JU) + (n - PAIRS + 1 + SC))
                for e in range(2):
                    mm = pe.matmul(score_ps[pair][:, e, lo:CH], k_sb[b][0:ROWSM, pair, jj * P:(jj + 1) * P],
                                   q_sb[b][0:ROWSM, 2 * pair + e, c * CH + lo:(c + 1) * CH], start=True, stop=True)
                mm.then_inc(scores_full, 1)

            def weigh(s, b, c, jj):
                j = before[c] + jj
                diag = jj - CT * c
                lo = P * max(0, diag)
                if jj == 0:
                    pe.wait_ge(out_copied, s * QC + (c + FREE))
                if diag >= 0:
                    pe.wait_ge(probs_masked, s * NDIAG + PAIRS * (CT * c + diag + 1))
                else:
                    pe.wait_ge(probs_done, s * (PAIRS * JU) + (PAIRS * (j + 1) + SC))
                for h in range(UH):
                    mm = pe.matmul(out_ps[VW * h:VW * (h + 1), lo:CH], v_sb[b][:, jj, h, :],
                                   probs[:, (PAIRS * j + h // 2) % PRING, h % 2, lo:CH],
                                   start=(jj == 0), stop=(jj == CT * (c + 1) - 1), skip_group_check=True)
                mm.then_inc(pv_done, 1)

            k = 0
            for c in range(QC):
                pe.wait_ge(loaded[0][c], 16 * 16)
                for es in ring_events(True, False)[before[c]:before[c + 1]]:
                    for event in es:
                        fill(event, None, 0, k, 0, 0, 0)
                        k += 1
            fill(("max_rows", QC - 1), None, 0, k, 0, 0, 0)

            def step(i, b, more):
                s = i * 2 + b
                base = s * step_len + first_len
                shift = first_len % RING
                k = 0
                events = ring_events(more, True)
                after = None
                for c in range(QC):
                    if more:
                        pe.wait_ge(loaded[1 - b][c], i * 256 + 256 * (b + 1))
                    pe.wait_ge(max_loaded[c % 2], s * 128 + 64 * (c // 2 + 1))
                    for jj in range(CT * (c + 1)):
                        todo = list(events[before[c] + jj])
                        for pair in range(PAIRS):
                            for event in todo[0:2]:
                                fill(event, s, base, k, shift, 1 - b, s * QC + QC)
                                k += 1
                            todo = todo[2:]
                            scores(s, b, c, jj, pair)
                        if after:
                            weigh(s, b, *after)
                        after = (c, jj)
                        for event in todo:
                            fill(event, s, base, k, shift, 1 - b, s * QC + QC)
                            k += 1
                weigh(s, b, *after)
                for event in events[-1]:
                    fill(event, s, base, k, shift, 1 - b, s * QC + QC)
                    k += 1

            all_steps(pe, step)


def feed(nc, x, w_comp, b_comp, w_gate, w_up, w_down, out, ctx_all, ident, minus_half):
    with ExitStack() as ctx:
        def sem(name):
            return ctx.enter_context(nc.semaphore(name))

        w_int = sbuf(nc, ctx, "w_int", [P, 3, MF * D], I32)
        w_f32 = sbuf(nc, ctx, "w_f32", [P, 3, MF * D])
        wc = sbuf(nc, ctx, "wc", [P, KD, D])
        wc_hi = sbuf(nc, ctx, "wc_hi", [P, KD, D], F32R)
        wc_lo = sbuf(nc, ctx, "wc_lo", [P, KD, D], F32R)
        gu_hi = sbuf(nc, ctx, "gu_hi", [P, 2, KD, FH], F32R)
        gu_lo = sbuf(nc, ctx, "gu_lo", [P, 2, KD, FH], F32R)
        wdT = sbuf(nc, ctx, "wdT", [P, MF, D])
        bc = sbuf(nc, ctx, "bc", [P, D])
        xr = sbuf(nc, ctx, "xr", [P, CT, D])
        xb = sbuf(nc, ctx, "xb", [P, CT, D])
        ctx_now = sbuf(nc, ctx, "ctx_now", [P, CT, D])
        cT_hi = sbuf(nc, ctx, "cT_hi", [P, KD, CH], F32R)
        cT_lo = sbuf(nc, ctx, "cT_lo", [P, KD, CH], F32R)
        x1 = sbuf(nc, ctx, "x1", [P, CT, D])
        x1_kept = sbuf(nc, ctx, "x1_kept", [P, CT, D])
        stats = sbuf(nc, ctx, "stats2", [P, CT, 6])
        meanvar = sbuf(nc, ctx, "meanvar2", [P, CT, 2])
        var_eps = sbuf(nc, ctx, "var_eps2", [P, CT])
        rstd = sbuf(nc, ctx, "rstd2", [P, CT])
        xn = sbuf(nc, ctx, "xn2", [P, CT, D])
        xT_hi = sbuf(nc, ctx, "x2T_hi", [P, KD, CH], F32R)
        xT_lo = sbuf(nc, ctx, "x2T_lo", [P, KD, CH], F32R)
        silu = sbuf(nc, ctx, "silu", [P, 2, CH])
        h = sbuf(nc, ctx, "h", [P, MF, CH])
        res = sbuf(nc, ctx, "res", [P, CT, D])
        t_ps = banks(nc, ctx, "turn_ps", 2)
        y_ps = banks(nc, ctx, "y_ps", 2)
        g_ps = banks(nc, ctx, "g_ps", 2)
        u_ps = banks(nc, ctx, "u_ps", 2)

        w_in = [sem(f"w_in{i}") for i in range(3)]
        wc_in, bc_in, x_in = sem("wc_in"), sem("bc_in"), sem("x2_in")
        w_cast, w_turned, w_kept, w_lo_kept = sem("w_cast"), sem("w_turned"), sem("w_kept"), sem("w_lo_kept")
        wc_hi_done, wc_lo_done = sem("wc_hi_done"), sem("wc_lo_done")
        ctx_copied, xb_done, x1_moved = sem("ctx_copied"), sem("xb_done"), sem("x1_moved")
        turned, hi_done, lo_done = sem("turned2"), sem("hi_done"), sem("lo_done")
        y_full, x1_done = sem("y_full"), sem("x1_done")
        stats_done, aggr_done, rstd_done, normed = sem("stats2_done"), sem("aggr2_done"), sem("rstd2_done"), sem("normed2")
        eps_added, passed = sem("eps2_added"), sem("passed2")
        gu_full, silu_done, h_done = sem("gu_full"), sem("silu_done"), sem("h_done")
        down_full, res_done, stored = sem("down_full"), sem("res_done"), sem("stored")

        block = ctx.enter_context(nc.Block())
        NPREP = 3 * MF * KD // CT

        def prep_bank(q):
            per = KD * MF // CT
            which, r = q // per, q % per
            if which < 2:
                blocks = [r * CT + i for i in range(CT)]
                srcs = [(m % MF) * D + (m // MF) * P for m in blocks]
                return which, srcs, blocks
            blocks = [r * CT + i for i in range(CT)]
            srcs = [(m % KD) * FH + (m // KD) * P for m in blocks]
            return which, srcs, blocks

        def prep_to(tile, which, r):
            if which < 2:
                return tile[:, which].rearrange("p k f -> p (k f)")[:, r * CH:(r + 1) * CH]
            return tile[:].rearrange("p m d -> p (m d)")[:, r * CH:(r + 1) * CH]

        PER = KD * MF // CT

        @block.sync
        def _(sp):
            def load_x(n):
                sp.dma_start(xr[:], x[bass.ds(n * CH, CH), :].rearrange("(t p) d -> p t d", p=P)).then_inc(x_in, 16)

            def store(n):
                sp.wait_ge(res_done, n * 2 + 2)
                sp.dma_start(out[bass.ds(n * CH, CH), :].rearrange("(t p) d -> p t d", p=P), res[:]).then_inc(stored, 16)

            sp.sem_inc(stored, FREE)
            sp.dma_start(wc[:], w_comp.rearrange("(k p) n -> p k n", p=P)).then_inc(wc_in, 16)
            load_x(0)
            for i, wi in enumerate((w_gate, w_up)):
                sp.dma_start(w_int[:, i, :].rearrange("p (m d) -> p m d", m=MF), wi.rearrange("(m p) d -> p m d", p=P)
                             ).then_inc(w_in[i], 16)
            sp.dma_start(w_int[:, 2, :].rearrange("p (k f) -> p k f", k=KD), w_down.rearrange("(k p) f -> p k f", p=P)
                         ).then_inc(w_in[2], 16)
            sp.dma_start(bc[:], b_comp.rearrange("(a d) -> a d", a=1).to_broadcast([P, D])).then_inc(bc_in, 16)
            sp.wait_ge(xb_done, 1)
            load_x(1)
            with sp.Fori(0, NCH - 2) as n:
                sp.wait_ge(xb_done, n + 2)
                load_x(n + 2)
                store(n)
            store(NCH - 2)
            store(NCH - 1)
            sp.wait_ge(stored, NCH * 16 + FREE)

        @block.gpsimd
        def _(pool):
            def take_ctx(n):
                if not isinstance(n, int) or n > 0:
                    wait_apart(pool, turned, n * (2 * KD) - KD, passed)
                pool.tensor_copy(ctx_now[:], ctx_all[:, bass.ds(n * CT, CT), :]).then_inc(ctx_copied, 1)

            def inverse_deviation(n):
                wait_apart(pool, aggr_done, n * CT + CT, passed)
                pool.tensor_scalar(var_eps[:], meanvar[:, :, 1], EPS, None, ALU.add).then_inc(eps_added, 1)
                pool.wait_ge(eps_added, n + 1)
                pool.tensor_tensor(rstd[:], var_eps[:], minus_half[:], ALU.pow).then_inc(rstd_done, 1)

            def add_bias(n):
                pool.wait_ge(x_in, n * 16 + 16)
                if not isinstance(n, int) or n > 0:
                    pool.wait_ge(x1_done, n * 2)
                pool.tensor_tensor(xb[:], xr[:], bc[:, None, :].to_broadcast([P, CT, D]), ALU.add).then_inc(xb_done, 1)

            def keep(n):
                pool.wait_ge(x1_done, n * 2 + 2)
                if not isinstance(n, int) or n > 0:
                    wait_apart(pool, res_done, n * 2, passed)
                pool.tensor_copy(x1_kept[:], x1[:]).then_inc(x1_moved, 1)

            pool.wait_ge(bc_in, 16)
            take_ctx(0)
            add_bias(0)
            take_ctx(1)
            inverse_deviation(0)
            add_bias(1)
            keep(0)
            with pool.Fori(0, NCH - 2) as n:
                take_ctx(n + 2)
                inverse_deviation(n + 1)
                add_bias(n + 2)
                keep(n + 1)
            inverse_deviation(NCH - 1)
            keep(NCH - 1)

        @block.scalar
        def _(act):
            def high(n, which, to):
                for k in range(KD):
                    act.wait_ge(turned, n * (2 * KD) + (which * KD + k + 1))
                    act.activation(to[:, k, :], t_ps[k][:], ACT.Copy).then_inc(hi_done, 1)

            def gate(n, m):
                act.wait_ge(gu_full, n * MF + (m + 1))
                act.activation(silu[:, m % 2, :], g_ps[m % 2][:], ACT.Silu, scale=W_SCALE).then_inc(silu_done, 1)

            act.wait_ge(wc_in, 16)
            act.activation(wc_hi[:], wc[:], ACT.Copy).then_inc(wc_hi_done, 1)
            for q in range(3 * PER):
                act.wait_ge(w_turned, q + 1)
                which, r = q // PER, q % PER
                act.activation(prep_to(gu_hi if which < 2 else wdT, which, r), g_ps[q % 2][:], ACT.Copy).then_inc(w_kept, 1)
            high(0, 0, cT_hi)
            high(0, 1, xT_hi)
            with act.Fori(0, NCH - 1) as n:
                gate(n, 0)
                high(n + 1, 0, cT_hi)
                for m in range(1, MF):
                    gate(n, m)
                high(n + 1, 1, xT_hi)
            for m in range(MF):
                gate(NCH - 1, m)

        @block.vector
        def _(dve):
            def low(n, which, to, hi):
                for k in range(KD):
                    dve.wait_ge(hi_done, n * (2 * KD) + (which * KD + k + 1))
                    dve.tensor_tensor(to[:, k, :], t_ps[k][:], hi[:, k, :].bitcast(F32), ALU.subtract).then_inc(lo_done, 1)

            def residual(n):
                dve.wait_ge(xb_done, n + 1)
                if not isinstance(n, int) or n > 0:
                    dve.wait_ge(x1_moved, n)
                for i in range(2):
                    dve.wait_ge(y_full, n * 2 + i + 1)
                    dve.tensor_tensor(x1[:, 2 * i:2 * i + 2, :], y_ps[i][:].rearrange("p (t d) -> p t d", d=D),
                                      xb[:, 2 * i:2 * i + 2, :], ALU.add).then_inc(x1_done, 1)

            def norm(n):
                dve.wait_ge(x1_done, n * 2 + 2)
                for t in range(CT):
                    dve.bn_stats(stats[:, t, :], x1[:, t, :]).then_inc(stats_done, 1)
                for t in range(CT):
                    wait_apart(dve, stats_done, n * CT + t + 1, passed)
                    dve.bn_aggr(meanvar[:, t, :], stats[:, t, :]).then_inc(aggr_done, 1)
                dve.wait_ge(rstd_done, n + 1)
                for t in range(CT):
                    dve.tensor_scalar(xn[:, t, :], x1[:, t, :], meanvar[:, t, 0:1], rstd[:, t:t + 1],
                                      ALU.subtract, ALU.mult).then_inc(normed, 1)

            def hidden(n, m):
                dve.wait_ge(silu_done, n * MF + (m + 1))
                dve.scalar_tensor_tensor(out=h[:, m, :], in0=u_ps[m % 2][:], scalar=W_SCALE, in1=silu[:, m % 2, :],
                                         op0=ALU.mult, op1=ALU.mult).then_inc(h_done, 1)

            def result(n):
                dve.wait_ge(x1_moved, n + 1)
                dve.wait_ge(stored, n * 16 + FREE)
                for i in range(2):
                    dve.wait_ge(down_full, n * 2 + i + 1)
                    dve.scalar_tensor_tensor(out=res[:, 2 * i:2 * i + 2, :], in0=y_ps[i][:].rearrange("p (t d) -> p t d", d=D),
                                             scalar=W_SCALE, in1=x1_kept[:, 2 * i:2 * i + 2, :],
                                             op0=ALU.mult, op1=ALU.add).then_inc(res_done, 1)

            for i in range(3):
                dve.wait_ge(w_in[i], 16)
                dve.tensor_copy(w_f32[:, i, :], w_int[:, i, :]).then_inc(w_cast, 1)
            dve.wait_ge(wc_hi_done, 1)
            dve.tensor_tensor(wc_lo[:], wc[:], wc_hi[:].bitcast(F32), ALU.subtract).then_inc(wc_lo_done, 1)
            for q in range(2 * PER):
                dve.wait_ge(w_kept, q + 1)
                which, r = q // PER, q % PER
                dve.tensor_tensor(prep_to(gu_lo, which, r), g_ps[q % 2][:], prep_to(gu_hi, which, r).bitcast(F32),
                                  ALU.subtract).then_inc(w_lo_kept, 1)
            low(0, 0, cT_lo, cT_hi)
            residual(0)
            norm(0)
            low(0, 1, xT_lo, xT_hi)
            with dve.Fori(0, NCH - 1) as n:
                hidden(n, 0)
                low(n + 1, 0, cT_lo, cT_hi)
                hidden(n, 1)
                hidden(n, 2)
                residual(n + 1)
                norm(n + 1)
                for m in range(3, MF):
                    hidden(n, m)
                low(n + 1, 1, xT_lo, xT_hi)
                result(n)
            for m in range(MF):
                hidden(NCH - 1, m)
            result(NCH - 1)

        @block.tensor
        def _(pe):
            def turn(n, which, src, ready, count):
                pe.wait_ge(ready, count)
                for k in range(KD):
                    for t in range(CT):
                        mm = pe.transpose(t_ps[k][:, t * P:(t + 1) * P], src[:, t, k * P:(k + 1) * P], ident[:])
                    mm.then_inc(turned, 1)

            def out_project(n):
                pe.wait_ge(lo_done, n * (2 * KD) + KD)
                terms = [(cT_hi, wc_hi), (cT_lo, wc_hi), (cT_hi, wc_lo)]
                for t in range(CT):
                    for i, (k, (cx, wx)) in enumerate([(k, t_) for k in range(KD) for t_ in terms]):
                        mm = pe.matmul(y_ps[t // 2][:, (t % 2) * D:(t % 2 + 1) * D], cx[:, k, t * P:(t + 1) * P],
                                       wx[:, k, :], start=(i == 0), stop=(i == 3 * KD - 1))
                    if t % 2:
                        mm.then_inc(y_full, 1)

            def gate_up(n, m):
                if m == 0:
                    pe.wait_ge(lo_done, n * (2 * KD) + 2 * KD)
                if m >= 2:
                    pe.wait_ge(h_done, n * MF + (m - 1))
                terms = [(gu_hi, xT_hi), (gu_lo, xT_hi), (gu_hi, xT_lo)]
                for which, bank in ((0, g_ps[m % 2]), (1, u_ps[m % 2])):
                    for i, (k, (wx, xx)) in enumerate([(k, t_) for k in range(KD) for t_ in terms]):
                        mm = pe.matmul(bank[:], wx[:, which, k, m * P:(m + 1) * P], xx[:, k, :],
                                       start=(i == 0), stop=(i == 3 * KD - 1))
                mm.then_inc(gu_full, 1)

            def down(n):
                pe.wait_ge(h_done, n * MF + MF)
                for t in range(CT):
                    for m in range(MF):
                        mm = pe.matmul(y_ps[t // 2][:, (t % 2) * D:(t % 2 + 1) * D], h[:, m, t * P:(t + 1) * P],
                                       wdT[:, m, :], start=(m == 0), stop=(m == MF - 1))
                    if t % 2:
                        mm.then_inc(down_full, 1)

            for q in range(3 * PER):
                which, srcs, _ = prep_bank(q)
                if q % PER == 0:
                    pe.wait_ge(w_cast, which + 1)
                if q >= 2:
                    if q - 2 < 2 * PER:
                        pe.wait_ge(w_lo_kept, q - 1)
                    else:
                        pe.wait_ge(w_kept, q - 1)
                for i, src in enumerate(srcs):
                    mm = pe.transpose(g_ps[q % 2][:, i * P:(i + 1) * P], w_f32[:, which, src:src + P], ident[:])
                mm.then_inc(w_turned, 1)
            turn(0, 0, ctx_now, ctx_copied, 1)
            pe.wait_ge(wc_lo_done, 1)
            out_project(0)
            turn(0, 1, xn, normed, CT)
            pe.wait_ge(w_lo_kept, 2 * PER)
            pe.wait_ge(w_kept, 3 * PER)
            with pe.Fori(0, NCH - 1) as n:
                gate_up(n, 0)
                turn(n + 1, 0, ctx_now, ctx_copied, n + 2)
                gate_up(n, 1)
                gate_up(n, 2)
                out_project(n + 1)
                for m in range(3, MF):
                    gate_up(n, m)
                turn(n + 1, 1, xn, normed, n * CT + 2 * CT)
                down(n)
            for m in range(MF):
                gate_up(NCH - 1, m)
            down(NCH - 1)


def layer(nc, x, w_exp, b_exp, w_comp, b_comp, w_gate, w_up, w_down, out):
    qk_scratch = nc.dram_tensor("qk_scratch", [2, 2 * D, TOK], F32, kind="Internal").ap()
    v_scratch = nc.dram_tensor("v_scratch", [TOK, D], F32, kind="Internal").ap()
    x2d = x.rearrange("b s d -> (b s) d")
    out2d = out.rearrange("b s d -> (b s) d")
    with ExitStack() as ctx:
        ident = sbuf(nc, ctx, "ident", [P, P])
        minus_half = sbuf(nc, ctx, "minus_half", [P, CT])
        ctx_all = sbuf(nc, ctx, "ctx_all", [P, TOK // P, D])
        project(nc, x2d, w_exp, b_exp, qk_scratch, v_scratch, ident, minus_half)
        attend(nc, qk_scratch, v_scratch, ctx_all, ident)
        feed(nc, x2d, w_comp, b_comp, w_gate, w_up, w_down, out2d, ctx_all, ident, minus_half)


_INS = ["L0_attn_x", "L0_attn_W_exp", "L0_attn_b_exp", "L0_attn_W_comp", "L0_attn_b_comp",
        "L0_ffn_w_gate", "L0_ffn_w_up", "L0_ffn_w_down"]


def kernel(**inputs):
    import numpy as np
    import concourse.bacc as bacc
    from concourse.bass_utils import run_bass_kernel_spmd

    nc = bacc.Bacc("TRN2", target_bir_lowering=False, num_devices=1)
    arrays, args = {}, []
    for name in _INS:
        a = np.ascontiguousarray(inputs[name])
        arrays[f"in_{name}"] = a
        args.append(nc.dram_tensor(f"in_{name}", a.shape, mybir.dt.from_np(a.dtype), kind="ExternalInput").ap())
    args.append(nc.dram_tensor("out_x", (B, S, D), F32, kind="ExternalOutput").ap())
    layer(nc, *args)
    r = run_bass_kernel_spmd(nc, [arrays], core_ids=[0])
    return r.results[0]["out_x"]
```

```python
import concourse.bass as bass
from concourse import mybir
from contextlib import ExitStack

F32 = mybir.dt.float32
F32R = mybir.dt.float32r
I32 = mybir.dt.int32
ALU = mybir.AluOpType
ACT = mybir.ActivationFunctionType
AX = mybir.AxisListType

P = 128
B, S, D = 2, 2048, 256
H = 16
HD = D // H
TOK = B * S
FH = 768
EPS = 1e-5
SCALE = HD ** -0.5
W_SCALE = 1.0 / 127.0

CH = 512
NCH = TOK // CH
CT = CH // P
KD = D // P
QKT = 2 * D // P
VB = D * CT // CH
MF = FH // P

QC = S // CH
KT = S // P
UH = 4
UG = H // UH
PAIRS = UH // 2
PAIR = 2 * HD
ROWS = 3 * PAIR
ROWSM = ROWS + 2
VW = 32
JU = sum(CT * (c + 1) for c in range(QC))
STEPS_BEFORE = [sum(CT * (a + 1) for a in range(c)) for c in range(QC + 1)]
LEAD = 20
QK_LOADS, V_LOADS = 9 * 16, 16
PRING = 8
RING = 3
NEG = -1.0e30
W_FIRST = 12
HB = 3
FREE = 1


def sbuf(nc, ctx, name, shape, dt=F32):
    return ctx.enter_context(nc.sbuf_tensor(name, shape, dt))


def wait_apart(eng, sem, count, passed):
    eng.wait_ge(sem, count)
    if not isinstance(count, int):
        eng.sem_inc(passed, 1)


def banks(nc, ctx, name, n):
    return [ctx.enter_context(nc.psum_tensor(f"{name}{i}", [P, CH], F32)) for i in range(n)]


class Operands:

    def __init__(self, nc, ctx, b):
        self.b = b
        self.q = sbuf(nc, ctx, f"q_sb{b}", [P, UH, S], F32R)
        self.k = sbuf(nc, ctx, f"k_sb{b}", [P, PAIRS, S], F32R)
        self.v = sbuf(nc, ctx, f"v_sb{b}", [P, KT, UH, VW])
        self.loaded = [ctx.enter_context(nc.semaphore(f"loaded{b}_{c}")) for c in range(QC)]
        self.v_loaded = [ctx.enter_context(nc.semaphore(f"v_loaded{b}_{c}")) for c in range(QC)]

    def load(self, sp, qk_scratch, v_scratch, g, c):
        b, here = self.b, slice(c * CH, (c + 1) * CH)
        toks = slice(b * S + c * CH, b * S + (c + 1) * CH)
        for r in range(3):
            for at, part in ((0, (0, 0, 1)[r]), (D, (0, 1, 0)[r])):
                rows = qk_scratch[part, bass.ds(g * (UH * HD) + at, UH * HD), toks]
                if at:
                    sp.dma_start(self.k[PAIR * r:PAIR * (r + 1), :, here].bitcast(F32),
                                 rows.rearrange("(pair r) t -> r pair t", r=PAIR)).then_inc(self.loaded[c], 16)
                else:
                    rows = rows.rearrange("(pair e r) t -> e r pair t", e=2, r=HD)
                    for e in range(2):
                        row = PAIR * r + HD * e
                        sp.dma_start(self.q[row:row + HD, e:UH:2, here].bitcast(F32), rows[e]).then_inc(self.loaded[c], 16)
        sp.dma_start(self.v[:, c * CT:(c + 1) * CT].rearrange("p t h d -> p t (h d)"),
                     v_scratch[toks, bass.ds(g * (UH * VW), UH * VW)].rearrange("(t p) f -> p t f", p=P)
                     ).then_inc(self.v_loaded[c], 16)


def project(nc, x, w_exp, b_exp, qk_scratch, v_scratch, qk_stored, v_stored, units, ident, minus_half):
    unit0, unit1 = units
    with ExitStack() as ctx:
        def sem(name):
            return ctx.enter_context(nc.semaphore(name))

        w = sbuf(nc, ctx, "w", [P, KD, 3 * D])
        w_hi = sbuf(nc, ctx, "w_hi", [P, KD, 3 * D], F32R)
        w_lo = sbuf(nc, ctx, "w_lo", [P, KD, 3 * D], F32R)
        bqk = sbuf(nc, ctx, "bqk", [P, QKT])
        bv = sbuf(nc, ctx, "bv", [P, D])
        xt = sbuf(nc, ctx, "xt", [P, CT, D])
        xn = sbuf(nc, ctx, "xn", [P, CT, D])
        stats = sbuf(nc, ctx, "stats", [P, CT, 6])
        meanvar = sbuf(nc, ctx, "meanvar", [P, CT, 2])
        var_eps = sbuf(nc, ctx, "var_eps", [P, CT])
        rstd = sbuf(nc, ctx, "rstd", [P, CT])
        xT_hi = sbuf(nc, ctx, "xT_hi", [P, 2, KD, CH], F32R)
        xT_lo = sbuf(nc, ctx, "xT_lo", [P, 2, KD, CH], F32R)
        qk_hi = unit1.q[:, 0, :].rearrange("p (m t) -> p m t", m=QKT)
        qk_lo = unit1.q[:, 1, :].rearrange("p (m t) -> p m t", m=QKT)
        vs = unit1.v[:].rearrange("p t h w -> p (t h w)").rearrange("p (t h w) -> p t h w", t=CT, h=H)
        t_ps = banks(nc, ctx, "xT_ps", KD)
        qk_ps = banks(nc, ctx, "qk_ps", QKT)
        v_ps = banks(nc, ctx, "v_ps", VB)

        w_in, b_in, x_in = sem("w_in"), sem("b_in"), sem("x_in")
        ident_set, ident_made, exponent_set = sem("ident_set"), sem("ident_made"), sem("exponent_set")
        w_hi_done, w_lo_done = sem("w_hi_done"), sem("w_lo_done")
        stats_done, aggr_done, rstd_done, normed = sem("stats_done"), sem("aggr_done"), sem("rstd_done"), sem("normed")
        eps_added, passed = sem("eps_added"), sem("passed")
        turned, xT_hi_done, xT_lo_done = sem("turned"), sem("xT_hi_done"), sem("xT_lo_done")
        qk_full, qk_hi_done, qk_lo_done = sem("qk_full"), sem("qk_hi_done"), sem("qk_lo_done")
        v_full, v_done = sem("v_full"), sem("v_done")
        q_zero, k_ones, v_zero, v_ones = sem("q_zero0"), sem("k_ones0"), sem("v_zero0"), sem("v_ones0")

        block = ctx.enter_context(nc.Block())

        @block.sync
        def _(sp):
            def load_x(n):
                sp.dma_start(xt[:], x[bass.ds(n * CH, CH), :].rearrange("(t p) d -> p t d", p=P)).then_inc(x_in, 16)

            def store(n):
                for m in range(QKT):
                    sp.wait_ge(qk_lo_done, n * QKT + (m + 1 + QKT))
                    for part, half in enumerate((qk_hi, qk_lo)):
                        sp.dma_start(qk_scratch[part, m * P:(m + 1) * P, bass.ds(n * CH, CH)],
                                     half[:, m, :].bitcast(F32)).then_inc(qk_stored[m], 16)
                sp.wait_ge(v_done, n * 2 + (2 + VB))
                sp.dma_start(v_scratch[bass.ds(n * CH, CH), :].rearrange("(t p) f -> p t f", p=P),
                             vs.rearrange("p t h w -> p t (h w)")).then_inc(v_stored, 16)

            for m in range(QKT):
                sp.sem_inc(qk_stored[m], FREE)
            sp.sem_inc(v_stored, FREE)
            load_x(0)
            sp.dma_start(w[:], w_exp.rearrange("(k p) n -> p k n", p=P)).then_inc(w_in, 16)
            sp.dma_start(bqk[:], b_exp[0:2 * D].rearrange("(m p) -> p m", p=P),
                         allow_slow_non_contiguous=True).then_inc(b_in, 16)
            sp.dma_start(bv[:], b_exp[2 * D:3 * D].rearrange("(a d) -> a d", a=1).to_broadcast([P, D])).then_inc(b_in, 16)
            for n in range(2):
                sp.wait_ge(normed, (n + 1) * CT)
                load_x(n + 1)
            with sp.Fori(0, QC) as n:
                sp.wait_ge(normed, (n + 3) * CT)
                load_x(n + 3)
                store(n)
            for m in range(QKT):
                sp.wait_ge(qk_stored[m], QC * 32 + FREE)
            sp.wait_ge(v_stored, QC * 16 + FREE)
            sp.wait_ge(q_zero, UH)
            sp.wait_ge(k_ones, 1)
            sp.wait_ge(normed, (NCH - 1) * CT)
            load_x(NCH - 1)
            for c in range(2):
                store(QC + c)
                unit0.load(sp, qk_scratch, v_scratch, 0, c)
            store(QC + 2)
            store(QC + 3)

        @block.gpsimd
        def _(pool):
            pool.memset(ident[:], 0.0).then_inc(ident_set, 1)
            pool.wait_ge(ident_set, 1)
            pool.affine_select(out=ident[:], in_=ident[:], compare_op=ALU.not_equal, fill=1.0, base=0,
                               pattern=[[-1, P]], channel_multiplier=1).then_inc(ident_made, 1)

            def inverse_deviation(n):
                wait_apart(pool, aggr_done, n * CT + CT, passed)
                pool.tensor_scalar(var_eps[:], meanvar[:, :, 1], EPS, None, ALU.add).then_inc(eps_added, 1)
                pool.wait_ge(eps_added, n + 1)
                pool.tensor_tensor(rstd[:], var_eps[:], minus_half[:], ALU.pow).then_inc(rstd_done, 1)

            pool.memset(minus_half[:], -0.5).then_inc(exponent_set, 1)
            pool.wait_ge(exponent_set, 1)
            pool.memset(vs, 0.0).then_inc(v_zero, 1)
            pool.wait_ge(v_zero, 1)
            pool.memset(vs[:, :, :, HD:HD + 1], 1.0).then_inc(v_ones, 1)
            pool.wait_ge(v_ones, 1)
            for n in range(2):
                inverse_deviation(n)
                for h in range(2 * n, 2 * n + 2):
                    pool.memset(unit0.q[0:ROWS, h].bitcast(F32), 0.0).then_inc(q_zero, 1)
            inverse_deviation(2)
            pool.wait_ge(q_zero, UH)
            pool.wait_ge(rstd_done, 3)
            pool.memset(unit0.k[ROWS:ROWSM].bitcast(F32), 1.0).then_inc(k_ones, 1)
            pool.wait_ge(k_ones, 1)
            inverse_deviation(3)
            with pool.Fori(0, NCH - QC) as n:
                inverse_deviation(n + QC)

        @block.scalar
        def _(act):
            def xT_high(n, b):
                for k in range(KD):
                    act.wait_ge(turned, n * KD + k + 1)
                    act.activation(xT_hi[:, b, k, :], t_ps[k][:], ACT.Copy).then_inc(xT_hi_done, 1)

            def qk_high(n):
                for m in range(QKT):
                    act.wait_ge(qk_full, n * QKT + m + 1)
                    act.wait_ge(qk_stored[m], n * 32 + FREE)
                    act.activation(qk_hi[:, m, :], qk_ps[m][:], ACT.Identity, bias=bqk[:, m:m + 1]
                                   ).then_inc(qk_hi_done, 1)

            act.wait_ge(w_in, 16)
            act.activation(w_hi[:], w[:], ACT.Copy).then_inc(w_hi_done, 1)
            act.wait_ge(b_in, 32)
            xT_high(0, 0)
            with act.Fori(0, NCH // 2 - 1) as i:
                for b in range(2):
                    xT_high(i * 2 + b + 1, 1 - b)
                    qk_high(i * 2 + b)
            xT_high(NCH - 1, 1)
            qk_high(NCH - 2)
            qk_high(NCH - 1)

        @block.vector
        def _(dve):
            def norm(n):
                dve.wait_ge(x_in, n * 16 + 16)
                for t in range(CT):
                    dve.bn_stats(stats[:, t, :], xt[:, t, :]).then_inc(stats_done, 1)
                for t in range(CT):
                    wait_apart(dve, stats_done, n * CT + t + 1, passed)
                    dve.bn_aggr(meanvar[:, t, :], stats[:, t, :]).then_inc(aggr_done, 1)
                dve.wait_ge(rstd_done, n + 1)
                for t in range(CT):
                    dve.tensor_scalar(xn[:, t, :], xt[:, t, :], meanvar[:, t, 0:1], rstd[:, t:t + 1],
                                      ALU.subtract, ALU.mult).then_inc(normed, 1)

            def xT_low(n, b):
                for k in range(KD):
                    dve.wait_ge(xT_hi_done, n * KD + k + 1)
                    dve.tensor_tensor(xT_lo[:, b, k, :], t_ps[k][:], xT_hi[:, b, k, :].bitcast(F32), ALU.subtract).then_inc(xT_lo_done, 1)

            def qkv_low(n):
                for m in range(QKT):
                    dve.wait_ge(qk_hi_done, n * QKT + m + 1)
                    dve.scalar_tensor_tensor(out=qk_lo[:, m, :], in0=qk_ps[m][:], scalar=bqk[:, m:m + 1],
                                             in1=qk_hi[:, m, :].bitcast(F32), op0=ALU.add, op1=ALU.subtract).then_inc(qk_lo_done, 1)
                dve.wait_ge(v_stored, n * 16 + FREE)
                for i in range(2):
                    dve.wait_ge(v_full, n * 2 + i + 1)
                    dve.tensor_tensor(vs[:, 2 * i:2 * i + 2, :, 0:HD], v_ps[i][:].rearrange("p (t h d) -> p t h d", h=H, d=HD),
                                      bv[:, None, :].to_broadcast([P, 2, D]).rearrange("p t (h d) -> p t h d", d=HD),
                                      ALU.add).then_inc(v_done, 1)

            dve.sem_inc(qk_lo_done, QKT)
            dve.sem_inc(v_done, VB)
            norm(0)
            dve.wait_ge(v_ones, 1)
            dve.wait_ge(w_hi_done, 1)
            dve.tensor_tensor(w_lo[:], w[:], w_hi[:].bitcast(F32), ALU.subtract).then_inc(w_lo_done, 1)
            dve.wait_ge(b_in, 32)
            xT_low(0, 0)
            norm(1)
            with dve.Fori(0, NCH // 2 - 1) as i:
                for b in range(2):
                    xT_low(i * 2 + b + 1, 1 - b)
                    norm(i * 2 + b + 2)
                    qkv_low(i * 2 + b)
            xT_low(NCH - 1, 1)
            qkv_low(NCH - 2)
            qkv_low(NCH - 1)

        @block.tensor
        def _(pe):
            def turn(n):
                if not isinstance(n, int) or n > 0:
                    pe.wait_ge(xT_lo_done, n * KD)
                pe.wait_ge(normed, n * CT + CT)
                for k in range(KD):
                    for t in range(CT):
                        mm = pe.transpose(t_ps[k][:, t * P:(t + 1) * P], xn[:, t, k * P:(k + 1) * P], ident[:])
                    mm.then_inc(turned, 1)

            terms = [(w_hi, xT_hi), (w_lo, xT_hi), (w_hi, xT_lo)]

            def project_chunk(n, b):
                pe.wait_ge(xT_lo_done, n * KD + KD)
                for m in range(QKT):
                    pe.wait_ge(qk_lo_done, n * QKT + (m + 1))
                    for i, (k, (wx, xx)) in enumerate([(k, t) for k in range(KD) for t in terms]):
                        mm = pe.matmul(qk_ps[m][:], wx[:, k, m * P:(m + 1) * P], xx[:, b, k, :],
                                       start=(i == 0), stop=(i == 3 * KD - 1))
                    mm.then_inc(qk_full, 1)
                for t in range(CT):
                    if t % 2 == 0:
                        pe.wait_ge(v_done, n * 2 + (t // 2 + 1))
                    for i, (k, (wx, xx)) in enumerate([(k, t_) for k in range(KD) for t_ in terms]):
                        mm = pe.matmul(v_ps[t // 2][:, (t % 2) * D:(t % 2 + 1) * D], xx[:, b, k, t * P:(t + 1) * P],
                                       wx[:, k, 2 * D:3 * D], start=(i == 0), stop=(i == 3 * KD - 1))
                    if t % 2:
                        mm.then_inc(v_full, 1)

            pe.wait_ge(ident_made, 1)
            turn(0)
            pe.wait_ge(w_lo_done, 1)
            with pe.Fori(0, NCH // 2 - 1) as i:
                for b in range(2):
                    turn(i * 2 + b + 1)
                    project_chunk(i * 2 + b, b)
            turn(NCH - 1)
            project_chunk(NCH - 2, 0)
            project_chunk(NCH - 1, 1)


def maxima_events():
    steps = []
    for c in range(QC):
        events = []
        for t in range(CT):
            events += [("scores", c, t, (h,), x) for h in range(UH) for x in range(c)]
            n = {0: UH, 1: 2 if c else 1}.get(t, 1)
            events += [("scores", c, t, tuple(range(h, h + n)), c) for h in range(0, UH, n)]
        at = [len(events) * i // (CT * (c + 1)) for i in range(CT * (c + 1) + 1)]
        steps += [events[lo:hi] for lo, hi in zip(at, at[1:])]
    return steps


def ring_events(first, last):
    maxima = maxima_events()
    steps = []
    for i in range(JU):
        u, a = divmod(i + LEAD, JU)
        now = [] if last and u else [(u, e) for e in maxima[a]]
        for c in range(QC):
            end, start = STEPS_BEFORE[c + 1] + 1, STEPS_BEFORE[c] + 2
            if a == end % JU and not (last and u - end // JU > 0):
                now.append((u - end // JU, ("max_rows", c)))
            if i == start and not (first and c == 0):
                now.append((0 if c else -1, ("ctx_rows", (c - 1) % QC)))
        steps.append(now)
    return steps


def first_events():
    maxima = maxima_events()
    return [[(0, e) for e in maxima[a]] + [(0, ("max_rows", c)) for c in range(QC) if a == STEPS_BEFORE[c + 1] + 1]
            for a in range(LEAD)]


def attend(nc, qk_scratch, v_scratch, qk_stored, v_stored, ctx_scratch, ctx_out, ctx_stored, w_gate, w_up, w_down,
           weights, ops, ident, load_next):
    with ExitStack() as ctx:
        def sem(name):
            return ctx.enter_context(nc.semaphore(name))

        gu_hi, gu_lo, wd_hi, wd_lo = weights
        probs = sbuf(nc, ctx, "probs", [P, PRING, 2, CH])
        mask = sbuf(nc, ctx, "mask", [P, P])
        mask_r = sbuf(nc, ctx, "mask_r", [P, P], F32R)
        ident_r = sbuf(nc, ctx, "ident_r", [P, P], F32R)
        part_max = sbuf(nc, ctx, "part_max", [P, 2, CT * UH, QC])
        row_max = sbuf(nc, ctx, "row_max", [P, 2, CT * UH])
        neg_max = sbuf(nc, ctx, "neg_max", [P, 2, CT * UH, 2])
        max_rows = sbuf(nc, ctx, "max_rows", [2 * UH, 2, CH], F32R)
        ctxT = sbuf(nc, ctx, "ctxT", [P, 2, CH])
        inv_sum = sbuf(nc, ctx, "inv_sum", [P, 2, CT * UH])
        ring = banks(nc, ctx, "ring", RING)
        score_ps = [ctx.enter_context(nc.psum_tensor(f"score_ps{p}", [P, 2, CH], F32)) for p in range(PAIRS)]
        out_ps = banks(nc, ctx, "out_ps", 1)[0]

        room = probs[:].rearrange("p n e q -> p (n e q)")
        WN = MF * D
        w_int = [room[:, 0:WN].bitcast(I32), room[:, WN:2 * WN].bitcast(I32)]
        w_f32, w_hi, w_lo = [room[:, (2 + i) * WN:(3 + i) * WN] for i in range(3)]
        W_BANKS = WN // CH
        score_banks = [score_ps[q // 2][:, q % 2, :] for q in range(2 * PAIRS)]

        q_zero, k_ones = sem("q_zero1"), sem("k_ones1")
        mask_zero, mask_made, mask_rounded = sem("mask_zero"), sem("mask_made"), sem("mask_rounded")
        w_in = [sem(f"w_in{i}") for i in range(3)]
        w_cast, w_rounded, w_rest, w_turned, w_kept = [sem(n) for n in ("w_cast", "w_rounded", "w_rest", "w_turned", "w_kept")]
        ring_full, ring_free, passed = sem("ring_full"), sem("ring_free"), sem("passed1")
        max_done, max_hi_done, max_split = sem("max_done"), sem("max_hi_done"), sem("max_split")
        max_loaded = [sem(f"max_loaded{i}") for i in range(2)]
        scores_full, probs_done, probs_masked = sem("scores_full"), sem("probs_done"), sem("probs_masked")
        pv_done, out_copied, inv_done = sem("pv_done"), sem("out_copied"), sem("inv_done")

        prologue = first_events()
        before_steps = sum(map(len, prologue))
        step_len = sum(map(len, ring_events(False, False)))
        last_events = sum(map(len, ring_events(False, True)))
        assert step_len % RING == 0 and sum(map(len, ring_events(True, False))) == step_len - 1
        NDIAG = CT * PAIRS
        before = STEPS_BEFORE
        ORDER = [(c, jj) for c in range(QC) for jj in range(CT * (c + 1))]
        LAG = 2
        SC, PC = PAIRS, PRING // PAIRS

        def ring_start(s):
            if isinstance(s, int) and s == 0:
                return before_steps
            return s * step_len + (before_steps - 1)

        def slot_base(first):
            return before_steps if first else before_steps - 1

        def in_step(unit, event, s, first=False, last=False):
            return ring_start(s) + ([e for now in ring_events(first, last) for e in now].index((unit, event)) + 1)

        def all_steps(eng, step):
            step(0, 0, True, False)
            with eng.Fori(0, UG - 1) as i:
                step(i, 1, False, False)
                step(i + 1, 0, False, False)
            step(UG - 1, 1, False, True)

        block = ctx.enter_context(nc.Block())

        @block.sync
        def _(sp):
            def place_max(b, c, through):
                sp.wait_ge(ring_free, through)
                for h in range(UH):
                    sp.dma_start(ops[b].q[ROWS:ROWSM, h, c * CH:(c + 1) * CH].bitcast(F32),
                                 max_rows[2 * h:2 * h + 2, c % 2, :].bitcast(F32)).then_inc(max_loaded[c % 2], 16)

            def store_ctx(i, b, c, through):
                wait_apart(sp, ring_free, through, passed)
                toks = slice(b * S + c * CH, b * S + (c + 1) * CH)
                to = ctx_scratch[toks, bass.ds(i * (UH * HD), UH * HD)].rearrange("(t p) f -> p t f", p=P)
                sp.dma_start(to, ctx_out[:, c % 2].rearrange("p (t h) d -> p t (h d)", h=UH)).then_inc(ctx_stored[c % 2], 16)

            def step(i, b, first, last):
                s = i * 2 + b
                if first:
                    sp.wait_ge(q_zero, 1)
                    sp.wait_ge(k_ones, 1)
                elif not last:
                    wait_apart(sp, pv_done, s * JU + PC, passed)
                chunk = 0
                for unit, event in (e for now in ring_events(first, last) for e in now):
                    kind, c = event[0], event[1]
                    if kind == "max_rows":
                        place_max(b ^ unit, c, in_step(unit, event, s, first, last))
                    if kind == "ctx_rows":
                        store_ctx(i + (b - 1 if unit else 0), b ^ -unit, c, in_step(unit, event, s, first, last))
                    if kind != "scores" and chunk < QC and not last:
                        ops[1 - b].load(sp, qk_scratch, v_scratch, i + b, chunk)
                        chunk += 1

            sp.dma_start(w_int[0].rearrange("p (m d) -> p m d", m=MF), w_gate.rearrange("(m p) d -> p m d", p=P)).then_inc(w_in[0], 16)
            sp.dma_start(w_int[1].rearrange("p (m d) -> p m d", m=MF), w_up.rearrange("(m p) d -> p m d", p=P)).then_inc(w_in[1], 16)
            for c in range(2, QC):
                ops[0].load(sp, qk_scratch, v_scratch, 0, c)
            sp.wait_ge(w_cast, 1)
            sp.dma_start(w_int[0].rearrange("p (k f) -> p k f", k=KD), w_down.rearrange("(k p) f -> p k f", p=P)).then_inc(w_in[2], 16)
            flat = [e for now in prologue for e in now]
            for k, (unit, event) in enumerate(flat):
                if event[0] == "max_rows":
                    place_max(0, event[1], k + 1)
            for m in range(QKT):
                sp.wait_ge(qk_stored[m], NCH * 32 + FREE)
            sp.wait_ge(v_stored, NCH * 16 + FREE)
            all_steps(sp, step)
            for i in range(2):
                sp.wait_ge(ctx_stored[i], 16 * sum(c % 2 == i for c in range(B * UG * QC - 1)))
            load_next(sp)
            store_ctx(UG - 1, 1, QC - 1, ring_start(2 * UG - 1) + last_events + 1)

        @block.gpsimd
        def _(pool):
            pool.memset(mask[:], 0.0).then_inc(mask_zero, 1)
            pool.wait_ge(mask_zero, 1)
            pool.affine_select(out=mask[:], in_=mask[:], compare_op=ALU.is_ge, fill=NEG,
                               base=0, pattern=[[-1, P]], channel_multiplier=1).then_inc(mask_made, 1)
            pool.wait_ge(mask_made, 1)
            for w in range(3):
                pool.wait_ge(w_in[w], 16)
                if w:
                    pool.wait_ge(w_rest, w)
                pool.tensor_copy(w_f32, w_int[w % 2]).then_inc(w_cast, 1)
                pool.wait_ge(w_rounded, w + 1)
                if w:
                    pool.wait_ge(w_turned, 2 * W_BANKS * w)
                pool.tensor_tensor(w_lo, w_f32, w_hi, ALU.subtract).then_inc(w_rest, 1)
            pool.wait_ge(w_rest, 3)
            for m in range(QKT):
                pool.wait_ge(qk_stored[m], NCH * 32 + FREE)
            pool.memset(ops[1].q[0:ROWS].bitcast(F32), 0.0).then_inc(q_zero, 1)
            pool.wait_ge(q_zero, 1)
            pool.memset(ops[1].k[ROWS:ROWSM].bitcast(F32), 1.0).then_inc(k_ones, 1)
            pool.wait_ge(k_ones, 1)

            def step(i, b, first, last):
                s = i * 2 + b
                for c in range(QC):
                    for r in range(CT):
                        j = before[c] + CT * c + r
                        for pair in range(PAIRS):
                            n = PAIRS * j + pair
                            wait_apart(pool, probs_done, s * (PAIRS * JU) + (n + 1 + SC), passed)
                            at = probs[:, n % PRING, :, P * r:P * (r + 1)]
                            pool.affine_select(out=at, in_=at, compare_op=ALU.is_ge, fill=0.0, base=0,
                                               pattern=[[0, 2], [1, P]], channel_multiplier=-1).then_inc(probs_masked, 1)

            all_steps(pool, step)

        @block.scalar
        def _(act):
            act.sem_inc(probs_done, SC)
            act.sem_inc(out_copied, FREE)
            for w in range(3):
                act.wait_ge(w_cast, w + 1)
                if w:
                    act.wait_ge(w_turned, 2 * W_BANKS * w)
                act.activation(w_hi.bitcast(F32R), w_f32, ACT.Copy).then_inc(w_rounded, 1)
                for part, to in enumerate([(gu_hi, gu_lo), (gu_hi, gu_lo), (wd_hi, wd_lo)][w]):
                    to = to[:, w].rearrange("p k f -> p (k f)") if w < 2 else to[:].rearrange("p m d -> p (m d)")
                    for r in range(W_BANKS):
                        q = (2 * w + part) * W_BANKS + r
                        act.wait_ge(w_turned, q + 1)
                        act.activation(to[:, r * CH:(r + 1) * CH], score_banks[q % 4], ACT.Copy).then_inc(w_kept, 1)

            def copy_out(u, c):
                act.wait_ge(pv_done, u * JU + (before[c + 1] + PC))
                if not (isinstance(u, int) and u * QC + c < 2):
                    act.wait_ge(inv_done, u * QC + (c - 1))
                act.activation(ctxT[:, c % 2, :], out_ps[:], ACT.Copy).then_inc(out_copied, 1)

            def step(i, b, first, last):
                s = i * 2 + b
                for c, jj in ORDER:
                    j = before[c] + jj
                    lo = P * max(0, jj - CT * c)
                    for pair in range(PAIRS):
                        n = PAIRS * j + pair
                        act.wait_ge(scores_full, s * (PAIRS * JU) + (n + 1))
                        if pair == 0:
                            act.wait_ge(pv_done, s * JU + (j + 1))
                        act.activation(probs[:, n % PRING, :, lo:CH], score_ps[pair][:, :, lo:CH], ACT.Exp,
                                       scale=SCALE).then_inc(probs_done, 1)
                    if jj == LAG - 1 and not (first and c == 0):
                        copy_out(*((s, c - 1) if c else (s - 1, QC - 1)))

            act.wait_ge(w_turned, 6 * W_BANKS)
            all_steps(act, step)
            copy_out(2 * UG - 1, QC - 1)

        @block.vector
        def _(dve):
            def take(u, event, k, start):
                kind, c = event[0], event[1]
                bank = ring[k % RING]
                dve.wait_ge(ring_full, start + 1)
                if kind == "scores":
                    _, _, t, heads, x = event
                    n = P * (t + 1) if x == c else CH
                    at = t * UH + heads[0]
                    dve.tensor_reduce(part_max[:, c % 2, at:at + len(heads), x],
                                      bank[:, 0:len(heads) * n].rearrange("p (h q) -> p h q", q=n), AX.X, ALU.max
                                      ).then_inc(ring_free, 1)
                    if (t, heads[-1], x) == (CT - 1, UH - 1, c):
                        m = u * QC + c
                        dve.wait_ge(ring_free, start + 1)
                        dve.tensor_reduce(row_max[:, c % 2, :], part_max[:, c % 2, :, 0:c + 1], AX.X, ALU.max
                                          ).then_inc(max_done, 1)
                        dve.wait_ge(max_done, m + 1)
                        dve.tensor_scalar(neg_max[:, c % 2, :, 0].bitcast(F32R), row_max[:, c % 2, :], -1.0, None, ALU.mult
                                          ).then_inc(max_hi_done, 1)
                        dve.wait_ge(max_hi_done, m + 1)
                        dve.scalar_tensor_tensor(out=neg_max[:, c % 2, :, 1], in0=row_max[:, c % 2, :], scalar=-1.0,
                                                 in1=neg_max[:, c % 2, :, 0], op0=ALU.mult, op1=ALU.subtract
                                                 ).then_inc(max_split, 1)
                elif kind == "max_rows":
                    if not (isinstance(u, int) and u * QC + c < 2):
                        dve.wait_ge(max_loaded[c % 2], u * 128 + 64 * (c // 2))
                    dve.tensor_copy(max_rows[:, c % 2, :], bank[0:2 * UH, :]).then_inc(ring_free, 1)
                else:
                    rows = bank[:].rearrange("p (n w) -> p n w", w=VW)
                    dve.reciprocal(inv_sum[:, c % 2], rows[:, :, HD]).then_inc(inv_done, 1)
                    if not (isinstance(u, int) and u * QC + c < 2):
                        dve.wait_ge(ctx_stored[c % 2], u * 32 + 16 * (c // 2))
                    dve.wait_ge(inv_done, u * QC + (c + 1))
                    dve.tensor_tensor(ctx_out[:, c % 2], rows[:, :, 0:HD],
                                      inv_sum[:, c % 2, :, None].to_broadcast([P, CT * UH, HD]), ALU.mult).then_inc(ring_free, 1)

            dve.tensor_copy(ident_r[:], ident[:]).then_inc(mask_rounded, 1)
            dve.wait_ge(mask_made, 1)
            dve.tensor_copy(mask_r[:], mask[:]).then_inc(mask_rounded, 1)
            for k, (unit, event) in enumerate(e for now in prologue for e in now):
                take(unit, event, k, k)

            def step(i, b, first, last):
                s = i * 2 + b
                for k, (unit, event) in enumerate(e for now in ring_events(first, last) for e in now):
                    take(s + unit, event, slot_base(first) + k, ring_start(s) + k)

            all_steps(dve, step)
            take(2 * UG - 1, ("ctx_rows", QC - 1), slot_base(False) + last_events, ring_start(2 * UG - 1) + last_events)

        @block.tensor
        def _(pe):
            pe.sem_inc(pv_done, PC)

            def fill(u, b, event, k, start):
                kind, c = event[0], event[1]
                bank = ring[k % RING]
                if not (isinstance(start, int) and start < RING):
                    pe.wait_ge(ring_free, start - (RING - 1))
                if kind == "scores":
                    _, _, t, heads, x = event
                    q, keys = ops[b].q, ops[b].k
                    q_at = c * CH + t * P
                    n = P * (t + 1) if x == c else CH
                    for e, h in enumerate(heads):
                        mm = pe.matmul(bank[:, e * n:(e + 1) * n], q[0:ROWS, h, q_at:q_at + P],
                                       keys[0:ROWS, h // 2, x * CH:x * CH + n], start=True, stop=True)
                        if x == c:
                            mm = pe.matmul(bank[:, (e + 1) * n - P:(e + 1) * n], ident_r[:], mask_r[:],
                                           start=False, stop=True, skip_group_check=True)
                elif kind == "max_rows":
                    pe.wait_ge(max_split, u * QC + (c + 1))
                    for t in range(CT):
                        mm = pe.transpose(bank[0:2 * UH, t * P:(t + 1) * P],
                                          neg_max[:, c % 2, t * UH:(t + 1) * UH, :].rearrange("p h x -> p (h x)"), ident[:])
                else:
                    pe.wait_ge(out_copied, u * QC + (c + 1 + FREE))
                    for t in range(CT):
                        mm = pe.transpose(bank[:, t * P:(t + 1) * P], ctxT[:, c % 2, t * P:(t + 1) * P], ident[:])
                mm.then_inc(ring_full, 1)

            def scores(s, b, c, jj, pair):
                n = PAIRS * (before[c] + jj) + pair
                lo = P * max(0, jj - CT * c)
                pe.wait_ge(probs_done, s * (PAIRS * JU) + (n - PAIRS + 1 + SC))
                for e in range(2):
                    mm = pe.matmul(score_ps[pair][:, e, lo:CH], ops[b].k[0:ROWSM, pair, jj * P:(jj + 1) * P],
                                   ops[b].q[0:ROWSM, 2 * pair + e, c * CH + lo:(c + 1) * CH], start=True, stop=True)
                mm.then_inc(scores_full, 1)

            def weigh(u, b, c, jj):
                j = before[c] + jj
                diag = jj - CT * c
                lo = P * max(0, diag)
                if diag == 0:
                    pe.wait_ge(ops[b].v_loaded[c], loads_of(u, b, V_LOADS))
                if jj == 0:
                    pe.wait_ge(out_copied, u * QC + (c + FREE))
                if diag >= 0:
                    pe.wait_ge(probs_masked, u * (QC * NDIAG) + (NDIAG * c + PAIRS * (diag + 1)))
                else:
                    pe.wait_ge(probs_done, u * (PAIRS * JU) + (PAIRS * (j + 1) + SC))
                for h in range(UH):
                    mm = pe.matmul(out_ps[VW * h:VW * (h + 1), lo:CH], ops[b].v[:, jj, h, :],
                                   probs[:, (PAIRS * j + h // 2) % PRING, h % 2, lo:CH],
                                   start=(jj == 0), stop=(jj == CT * (c + 1) - 1), skip_group_check=True)
                mm.then_inc(pv_done, 1)

            def loads_of(u, b, dmas):
                return u * (dmas // 2) + (dmas // 2) * (2 - b)

            def turn_weights(q):
                w, part, r = q // (2 * W_BANKS), q // W_BANKS % 2, q % W_BANKS
                if r == 0:
                    pe.wait_ge(w_rest if part else w_rounded, w + 1)
                if q >= len(score_banks):
                    pe.wait_ge(w_kept, q - len(score_banks) + 1)
                for a in range(CT):
                    block_ = r * CT + a
                    at = (block_ % MF) * D + (block_ // MF) * P if w < 2 else (block_ % KD) * FH + (block_ // KD) * P
                    mm = pe.transpose(score_banks[q % 4][:, a * P:(a + 1) * P], (w_lo if part else w_hi)[:, at:at + P], ident[:])
                mm.then_inc(w_turned, 1)

            pe.wait_ge(mask_rounded, 2)
            k = q = 0
            for (c, jj), now in zip(ORDER, prologue):
                if jj == 0:
                    pe.wait_ge(ops[0].loaded[c], QK_LOADS)
                for unit, event in now:
                    fill(0, 0, event, k, k)
                    k += 1
                    while q < 6 * W_BANKS and k >= W_FIRST + (before_steps - W_FIRST) * q // (6 * W_BANKS):
                        turn_weights(q)
                        q += 1
            pe.wait_ge(w_kept, 6 * W_BANKS)

            def step(i, b, first, last):
                s = i * 2 + b
                pending = [] if first else [(s - 1, 1 - b, *ORDER[a - LAG]) for a in range(LAG)]
                k = 0

                def fills(events):
                    nonlocal k
                    for unit, event in events:
                        fill(s + unit, b ^ (unit == 1), event, slot_base(first) + k, ring_start(s) + k)
                        k += 1

                for j, ((c, jj), now) in enumerate(zip(ORDER, ring_events(first, last))):
                    ahead, a = divmod(j + LEAD, JU)
                    if ORDER[a][1] == 0 and not (last and ahead):
                        buffer = b ^ ahead
                        pe.wait_ge(ops[buffer].loaded[ORDER[a][0]], loads_of(s + ahead, buffer, QK_LOADS))
                    if jj == 0:
                        pe.wait_ge(max_loaded[c % 2], s * 128 + 64 * (c // 2 + 1))
                    pending.append((s, b, c, jj))
                    scores(s, b, c, jj, 0)
                    fills(now[0:1])
                    scores(s, b, c, jj, 1)
                    fills(now[1:3])
                    if len(pending) > LAG:
                        weigh(*pending.pop(0))
                    fills(now[3:])

            all_steps(pe, step)
            for a in range(LAG):
                weigh(2 * UG - 1, 1, *ORDER[a - LAG])
            fill(2 * UG - 1, 1, ("ctx_rows", QC - 1), slot_base(False) + last_events, ring_start(2 * UG - 1) + last_events)


class FirstLoads:

    def __init__(self, nc, ctx, x, w_comp, b_comp, ctx_scratch):
        self.wc = sbuf(nc, ctx, "wc", [P, KD, D])
        self.bc = sbuf(nc, ctx, "bc", [P, D])
        self.xr = sbuf(nc, ctx, "xr", [P, CT, D])
        self.ctx_now = sbuf(nc, ctx, "ctx_now", [P, CT, D])
        self.wc_in, self.bc_in, self.x_in, self.ctx_in = [
            ctx.enter_context(nc.semaphore(name)) for name in ("wc_in", "bc_in", "x2_in", "ctx_in")]
        self.x, self.w_comp, self.b_comp, self.ctx_scratch = x, w_comp, b_comp, ctx_scratch

    def load_x(self, sp, n):
        sp.dma_start(self.xr[:], self.x[bass.ds(n * CH, CH), :].rearrange("(t p) d -> p t d", p=P)).then_inc(self.x_in, 16)

    def load_ctx(self, sp, n):
        sp.dma_start(self.ctx_now[:], self.ctx_scratch[bass.ds(n * CH, CH), :].rearrange("(t p) d -> p t d", p=P)
                     ).then_inc(self.ctx_in, 16)

    def start(self, sp):
        sp.dma_start(self.wc[:], self.w_comp.rearrange("(k p) n -> p k n", p=P)).then_inc(self.wc_in, 16)
        self.load_ctx(sp, 0)
        self.load_x(sp, 0)
        sp.dma_start(self.bc[:], self.b_comp.rearrange("(a d) -> a d", a=1).to_broadcast([P, D])).then_inc(self.bc_in, 16)


def feed(nc, first, out, ctx_stored, weights, ident, minus_half):
    with ExitStack() as ctx:
        def sem(name):
            return ctx.enter_context(nc.semaphore(name))

        wc, bc, xr, ctx_now = first.wc, first.bc, first.xr, first.ctx_now
        wc_in, bc_in, x_in, ctx_in = first.wc_in, first.bc_in, first.x_in, first.ctx_in
        gu_hi, gu_lo, wd_hi, wd_lo = weights
        wc_hi = sbuf(nc, ctx, "wc_hi", [P, KD, D], F32R)
        wc_lo = sbuf(nc, ctx, "wc_lo", [P, KD, D], F32R)
        xb = sbuf(nc, ctx, "xb", [P, CT, D])
        cT_hi = sbuf(nc, ctx, "cT_hi", [P, KD, CH], F32R)
        cT_lo = sbuf(nc, ctx, "cT_lo", [P, KD, CH], F32R)
        x1 = sbuf(nc, ctx, "x1", [P, CT, D])
        x1_kept = sbuf(nc, ctx, "x1_kept", [P, CT, D])
        stats = sbuf(nc, ctx, "stats2", [P, CT, 6])
        meanvar = sbuf(nc, ctx, "meanvar2", [P, CT, 2])
        var_eps = sbuf(nc, ctx, "var_eps2", [P, CT])
        rstd = sbuf(nc, ctx, "rstd2", [P, CT])
        xn = sbuf(nc, ctx, "xn2", [P, CT, D])
        xT_hi = sbuf(nc, ctx, "x2T_hi", [P, KD, CH], F32R)
        xT_lo = sbuf(nc, ctx, "x2T_lo", [P, KD, CH], F32R)
        silu = sbuf(nc, ctx, "silu", [P, 2, CH])
        h = sbuf(nc, ctx, "h", [P, HB, CH])
        h_hi = sbuf(nc, ctx, "h_hi", [P, MF, CH], F32R)
        h_lo = sbuf(nc, ctx, "h_lo", [P, MF, CH], F32R)
        res = sbuf(nc, ctx, "res", [P, CT, D])
        t_ps = banks(nc, ctx, "turn_ps", 2)
        y_ps = banks(nc, ctx, "y_ps", 2)
        g_ps = banks(nc, ctx, "g_ps", 2)
        u_ps = banks(nc, ctx, "u_ps", 2)

        wc_hi_done, wc_lo_done = sem("wc_hi_done"), sem("wc_lo_done")
        xb_done, x1_moved = sem("xb_done"), sem("x1_moved")
        turned, hi_done, lo_done = sem("turned2"), sem("hi_done"), sem("lo_done")
        y_full, x1_done = sem("y_full"), sem("x1_done")
        stats_done, aggr_done, rstd_done, normed = sem("stats2_done"), sem("aggr2_done"), sem("rstd2_done"), sem("normed2")
        eps_added, passed = sem("eps2_added"), sem("passed2")
        gu_full, silu_done, h_done = sem("gu_full"), sem("silu_done"), sem("h_done")
        h_hi_done, h_lo_done = sem("h_hi_done"), sem("h_lo_done")
        down_full, res_done, stored = sem("down_full"), sem("res_done"), sem("stored")

        block = ctx.enter_context(nc.Block())

        @block.sync
        def _(sp):
            def store(n):
                sp.wait_ge(res_done, n * 2 + 2)
                sp.dma_start(out[bass.ds(n * CH, CH), :].rearrange("(t p) d -> p t d", p=P), res[:]).then_inc(stored, 16)

            def load(n):
                sp.wait_ge(turned, n * (2 * KD) - KD)
                first.load_ctx(sp, n)
                sp.wait_ge(xb_done, n)
                first.load_x(sp, n)

            sp.sem_inc(stored, FREE)
            load(1)
            with sp.Fori(0, QC - 2) as n:
                load(n + 2)
                store(n)
            for i in range(2):
                sp.wait_ge(ctx_stored[i], B * UG * QC * 8)
            with sp.Fori(QC - 2, NCH - 2) as n:
                load(n + 2)
                store(n)
            store(NCH - 2)
            store(NCH - 1)
            sp.wait_ge(stored, NCH * 16 + FREE)

        @block.gpsimd
        def _(pool):
            def inverse_deviation(n):
                wait_apart(pool, aggr_done, n * CT + CT, passed)
                pool.tensor_scalar(var_eps[:], meanvar[:, :, 1], EPS, None, ALU.add).then_inc(eps_added, 1)
                pool.wait_ge(eps_added, n + 1)
                pool.tensor_tensor(rstd[:], var_eps[:], minus_half[:], ALU.pow).then_inc(rstd_done, 1)

            def add_bias(n):
                pool.wait_ge(x_in, n * 16 + 16)
                if not isinstance(n, int) or n > 0:
                    pool.wait_ge(x1_done, n * 2)
                pool.tensor_tensor(xb[:], xr[:], bc[:, None, :].to_broadcast([P, CT, D]), ALU.add).then_inc(xb_done, 1)

            def keep(n):
                pool.wait_ge(x1_done, n * 2 + 2)
                if not isinstance(n, int) or n > 0:
                    wait_apart(pool, res_done, n * 2, passed)
                pool.tensor_copy(x1_kept[:], x1[:]).then_inc(x1_moved, 1)

            pool.wait_ge(bc_in, 16)
            add_bias(0)
            inverse_deviation(0)
            add_bias(1)
            keep(0)
            with pool.Fori(0, NCH - 2) as n:
                inverse_deviation(n + 1)
                add_bias(n + 2)
                keep(n + 1)
            inverse_deviation(NCH - 1)
            keep(NCH - 1)

        @block.scalar
        def _(act):
            def high(n, which, to):
                for k in range(KD):
                    act.wait_ge(turned, n * (2 * KD) + (which * KD + k + 1))
                    act.activation(to[:, k, :], t_ps[k][:], ACT.Copy).then_inc(hi_done, 1)

            def gate(n, m):
                act.wait_ge(gu_full, n * MF + (m + 1))
                act.activation(silu[:, m % 2, :], g_ps[m % 2][:], ACT.Silu, scale=W_SCALE).then_inc(silu_done, 1)

            def hidden_high(n, m):
                act.wait_ge(h_done, n * MF + (m + 1))
                act.activation(h_hi[:, m, :], h[:, m % HB, :], ACT.Copy).then_inc(h_hi_done, 1)

            act.wait_ge(wc_in, 16)
            act.activation(wc_hi[:], wc[:], ACT.Copy).then_inc(wc_hi_done, 1)
            high(0, 0, cT_hi)
            high(0, 1, xT_hi)
            with act.Fori(0, NCH - 1) as n:
                gate(n, 0)
                high(n + 1, 0, cT_hi)
                for m in range(1, MF):
                    gate(n, m)
                    hidden_high(n, m - 1)
                hidden_high(n, MF - 1)
                high(n + 1, 1, xT_hi)
            gate(NCH - 1, 0)
            for m in range(1, MF):
                gate(NCH - 1, m)
                hidden_high(NCH - 1, m - 1)
            hidden_high(NCH - 1, MF - 1)

        @block.vector
        def _(dve):
            def low(n, which, to, hi):
                for k in range(KD):
                    dve.wait_ge(hi_done, n * (2 * KD) + (which * KD + k + 1))
                    dve.tensor_tensor(to[:, k, :], t_ps[k][:], hi[:, k, :].bitcast(F32), ALU.subtract).then_inc(lo_done, 1)

            def residual(n):
                dve.wait_ge(xb_done, n + 1)
                if not isinstance(n, int) or n > 0:
                    dve.wait_ge(x1_moved, n)
                for i in range(2):
                    dve.wait_ge(y_full, n * 2 + i + 1)
                    dve.tensor_tensor(x1[:, 2 * i:2 * i + 2, :], y_ps[i][:].rearrange("p (t d) -> p t d", d=D),
                                      xb[:, 2 * i:2 * i + 2, :], ALU.add).then_inc(x1_done, 1)

            def norm(n):
                dve.wait_ge(x1_done, n * 2 + 2)
                for t in range(CT):
                    dve.bn_stats(stats[:, t, :], x1[:, t, :]).then_inc(stats_done, 1)
                for t in range(CT):
                    wait_apart(dve, stats_done, n * CT + t + 1, passed)
                    dve.bn_aggr(meanvar[:, t, :], stats[:, t, :]).then_inc(aggr_done, 1)
                dve.wait_ge(rstd_done, n + 1)
                for t in range(CT):
                    dve.tensor_scalar(xn[:, t, :], x1[:, t, :], meanvar[:, t, 0:1], rstd[:, t:t + 1],
                                      ALU.subtract, ALU.mult).then_inc(normed, 1)

            def hidden(n, m):
                dve.wait_ge(h_lo_done, n * MF + (m + 1))
                dve.wait_ge(silu_done, n * MF + (m + 1))
                dve.scalar_tensor_tensor(out=h[:, m % HB, :], in0=u_ps[m % 2][:], scalar=W_SCALE, in1=silu[:, m % 2, :],
                                         op0=ALU.mult, op1=ALU.mult).then_inc(h_done, 1)

            def hidden_low(n, m):
                dve.wait_ge(h_hi_done, n * MF + (m + 1))
                dve.tensor_tensor(h_lo[:, m, :], h[:, m % HB, :], h_hi[:, m, :].bitcast(F32), ALU.subtract).then_inc(h_lo_done, 1)

            def result(n):
                dve.wait_ge(x1_moved, n + 1)
                dve.wait_ge(stored, n * 16 + FREE)
                for i in range(2):
                    dve.wait_ge(down_full, n * 2 + i + 1)
                    dve.scalar_tensor_tensor(out=res[:, 2 * i:2 * i + 2, :], in0=y_ps[i][:].rearrange("p (t d) -> p t d", d=D),
                                             scalar=W_SCALE, in1=x1_kept[:, 2 * i:2 * i + 2, :],
                                             op0=ALU.mult, op1=ALU.add).then_inc(res_done, 1)

            dve.sem_inc(h_lo_done, HB)
            dve.wait_ge(wc_hi_done, 1)
            dve.tensor_tensor(wc_lo[:], wc[:], wc_hi[:].bitcast(F32), ALU.subtract).then_inc(wc_lo_done, 1)
            low(0, 0, cT_lo, cT_hi)
            residual(0)
            norm(0)
            low(0, 1, xT_lo, xT_hi)
            with dve.Fori(0, NCH - 1) as n:
                hidden(n, 0)
                low(n + 1, 0, cT_lo, cT_hi)
                hidden(n, 1)
                hidden_low(n, 0)
                hidden(n, 2)
                hidden_low(n, 1)
                residual(n + 1)
                norm(n + 1)
                for m in range(3, MF):
                    hidden(n, m)
                    hidden_low(n, m - 1)
                hidden_low(n, MF - 1)
                low(n + 1, 1, xT_lo, xT_hi)
                result(n)
            hidden(NCH - 1, 0)
            for m in range(1, MF):
                hidden(NCH - 1, m)
                hidden_low(NCH - 1, m - 1)
            hidden_low(NCH - 1, MF - 1)
            result(NCH - 1)

        @block.tensor
        def _(pe):
            def turn(n, which, src, ready, count):
                pe.wait_ge(ready, count)
                for k in range(KD):
                    for t in range(CT):
                        mm = pe.transpose(t_ps[k][:, t * P:(t + 1) * P], src[:, t, k * P:(k + 1) * P], ident[:])
                    mm.then_inc(turned, 1)

            def out_project(n):
                pe.wait_ge(lo_done, n * (2 * KD) + KD)
                terms = [(cT_hi, wc_hi), (cT_lo, wc_hi), (cT_hi, wc_lo)]
                for t in range(CT):
                    for i, (k, (cx, wx)) in enumerate([(k, t_) for k in range(KD) for t_ in terms]):
                        mm = pe.matmul(y_ps[t // 2][:, (t % 2) * D:(t % 2 + 1) * D], cx[:, k, t * P:(t + 1) * P],
                                       wx[:, k, :], start=(i == 0), stop=(i == 3 * KD - 1))
                    if t % 2:
                        mm.then_inc(y_full, 1)

            def gate_up(n, m):
                if m == 0:
                    pe.wait_ge(lo_done, n * (2 * KD) + 2 * KD)
                if m >= 2:
                    pe.wait_ge(h_done, n * MF + (m - 1))
                terms = [(gu_hi, xT_hi), (gu_lo, xT_hi), (gu_hi, xT_lo)]
                for which, bank in ((0, g_ps[m % 2]), (1, u_ps[m % 2])):
                    for i, (k, (wx, xx)) in enumerate([(k, t_) for k in range(KD) for t_ in terms]):
                        mm = pe.matmul(bank[:], wx[:, which, k, m * P:(m + 1) * P], xx[:, k, :],
                                       start=(i == 0), stop=(i == 3 * KD - 1))
                mm.then_inc(gu_full, 1)

            def down(n):
                pe.wait_ge(h_lo_done, n * MF + (MF + HB))
                terms = [(h_hi, wd_hi), (h_lo, wd_hi), (h_hi, wd_lo)]
                for t in range(CT):
                    for i, (m, (hx, wx)) in enumerate([(m, t_) for m in range(MF) for t_ in terms]):
                        mm = pe.matmul(y_ps[t // 2][:, (t % 2) * D:(t % 2 + 1) * D], hx[:, m, t * P:(t + 1) * P],
                                       wx[:, m, :], start=(i == 0), stop=(i == 3 * MF - 1))
                    if t % 2:
                        mm.then_inc(down_full, 1)

            turn(0, 0, ctx_now, ctx_in, 16)
            pe.wait_ge(wc_lo_done, 1)
            out_project(0)
            turn(0, 1, xn, normed, CT)
            with pe.Fori(0, NCH - 1) as n:
                gate_up(n, 0)
                turn(n + 1, 0, ctx_now, ctx_in, n * 16 + 32)
                gate_up(n, 1)
                gate_up(n, 2)
                out_project(n + 1)
                for m in range(3, MF):
                    gate_up(n, m)
                turn(n + 1, 1, xn, normed, n * CT + 2 * CT)
                down(n)
            for m in range(MF):
                gate_up(NCH - 1, m)
            down(NCH - 1)


def layer(nc, x, w_exp, b_exp, w_comp, b_comp, w_gate, w_up, w_down, out):
    qk_scratch = nc.dram_tensor("qk_scratch", [2, 2 * D, TOK], F32, kind="Internal").ap()
    v_scratch = nc.dram_tensor("v_scratch", [TOK, H * VW], F32, kind="Internal").ap()
    ctx_scratch = nc.dram_tensor("ctx_scratch", [TOK, D], F32, kind="Internal").ap()
    x2d = x.rearrange("b s d -> (b s) d")
    out2d = out.rearrange("b s d -> (b s) d")
    with ExitStack() as ctx:
        ident = sbuf(nc, ctx, "ident", [P, P])
        minus_half = sbuf(nc, ctx, "minus_half", [P, CT])
        weights = (sbuf(nc, ctx, "gu_hi", [P, 2, KD, FH], F32R), sbuf(nc, ctx, "gu_lo", [P, 2, KD, FH], F32R),
                   sbuf(nc, ctx, "wd_hi", [P, MF, D], F32R), sbuf(nc, ctx, "wd_lo", [P, MF, D], F32R))
        first = FirstLoads(nc, ctx, x2d, w_comp, b_comp, ctx_scratch)
        ctx_out = sbuf(nc, ctx, "ctx_out", [P, 2, CT * UH, HD])
        ctx_stored = [ctx.enter_context(nc.semaphore(f"ctx_stored{i}")) for i in range(2)]
        with ExitStack() as inner:
            units = [Operands(nc, inner, b) for b in range(B)]
            qk_stored = [inner.enter_context(nc.semaphore(f"qk_stored{m}")) for m in range(QKT)]
            v_stored = inner.enter_context(nc.semaphore("v_stored"))
            project(nc, x2d, w_exp, b_exp, qk_scratch, v_scratch, qk_stored, v_stored, units, ident, minus_half)
            attend(nc, qk_scratch, v_scratch, qk_stored, v_stored, ctx_scratch, ctx_out, ctx_stored,
                   w_gate, w_up, w_down, weights, units, ident, first.start)
        feed(nc, first, out2d, ctx_stored, weights, ident, minus_half)


_INS = ["L0_attn_x", "L0_attn_W_exp", "L0_attn_b_exp", "L0_attn_W_comp", "L0_attn_b_comp",
        "L0_ffn_w_gate", "L0_ffn_w_up", "L0_ffn_w_down"]


def kernel(**inputs):
    import numpy as np
    import concourse.bacc as bacc
    from concourse.bass_utils import run_bass_kernel_spmd

    nc = bacc.Bacc("TRN2", target_bir_lowering=False, num_devices=1)
    arrays, args = {}, []
    for name in _INS:
        a = np.ascontiguousarray(inputs[name])
        arrays[f"in_{name}"] = a
        args.append(nc.dram_tensor(f"in_{name}", a.shape, mybir.dt.from_np(a.dtype), kind="ExternalInput").ap())
    args.append(nc.dram_tensor("out_x", (B, S, D), F32, kind="ExternalOutput").ap())
    layer(nc, *args)
    r = run_bass_kernel_spmd(nc, [arrays], core_ids=[0])
    return r.results[0]["out_x"]
```

```python
import concourse.bass as bass
from concourse import mybir
from contextlib import ExitStack

F32 = mybir.dt.float32
F32R = mybir.dt.float32r
BF16 = mybir.dt.bfloat16
I32 = mybir.dt.int32
ALU = mybir.AluOpType
ACT = mybir.ActivationFunctionType
AX = mybir.AxisListType

P = 128
B, S, D = 2, 2048, 256
H = 16
HD = D // H
TOK = B * S
FH = 768
EPS = 1e-5
SCALE = HD ** -0.5
W_SCALE = 1.0 / 127.0

CH = 512
NCH = TOK // CH
CT = CH // P
KD = D // P
QKT = 2 * D // P
VB = D * CT // CH
MF = FH // P

QC = S // CH
KT = S // P
UH = 4
UG = H // UH
PAIRS = UH // 2
PAIR = 2 * HD
ROWS = 3 * PAIR
ROWSM = ROWS + 2
VW = 32
JU = sum(CT * (c + 1) for c in range(QC))
STEPS_BEFORE = [sum(CT * (a + 1) for a in range(c)) for c in range(QC + 1)]
LEAD = 22
QK_LOADS, V_LOADS = 9 * 16, 16
PRING = 8
RING = 3
NEG = -1.0e30
W_FIRST = 20
HB = 3
FREE = 1


def sbuf(nc, ctx, name, shape, dt=F32):
    return ctx.enter_context(nc.sbuf_tensor(name, shape, dt))


def wait_apart(eng, sem, count, passed):
    eng.wait_ge(sem, count)
    if not isinstance(count, int):
        eng.sem_inc(passed, 1)


def banks(nc, ctx, name, n):
    return [ctx.enter_context(nc.psum_tensor(f"{name}{i}", [P, CH], F32)) for i in range(n)]


class Operands:

    def __init__(self, nc, ctx, b):
        self.b = b
        self.q = sbuf(nc, ctx, f"q_sb{b}", [P, UH, S], F32R)
        self.k = sbuf(nc, ctx, f"k_sb{b}", [P, PAIRS, S], F32R)
        self.v = sbuf(nc, ctx, f"v_sb{b}", [P, KT, UH, VW])
        self.loaded = [ctx.enter_context(nc.semaphore(f"loaded{b}_{c}")) for c in range(QC)]
        self.v_loaded = [ctx.enter_context(nc.semaphore(f"v_loaded{b}_{c}")) for c in range(QC)]

    def load(self, sp, qk_scratch, v_scratch, g, c):
        b, here = self.b, slice(c * CH, (c + 1) * CH)
        toks = slice(b * S + c * CH, b * S + (c + 1) * CH)
        for r in range(3):
            for at, part in ((0, (0, 0, 1)[r]), (D, (0, 1, 0)[r])):
                rows = qk_scratch[part, bass.ds(g * (UH * HD) + at, UH * HD), toks]
                if at:
                    sp.dma_start(self.k[PAIR * r:PAIR * (r + 1), :, here].bitcast(F32),
                                 rows.rearrange("(pair r) t -> r pair t", r=PAIR)).then_inc(self.loaded[c], 16)
                else:
                    rows = rows.rearrange("(pair e r) t -> e r pair t", e=2, r=HD)
                    for e in range(2):
                        row = PAIR * r + HD * e
                        sp.dma_start(self.q[row:row + HD, e:UH:2, here].bitcast(F32), rows[e]).then_inc(self.loaded[c], 16)
        sp.dma_start(self.v[:, c * CT:(c + 1) * CT, :, 0:HD].rearrange("p t h d -> p (t h) d"),
                     v_scratch[b * QC + c, bass.ds(g * P, P), :].rearrange("p (n d) -> p n d", d=HD)
                     ).then_inc(self.v_loaded[c], 16)


def project(nc, x, w_exp, b_exp, qk_scratch, v_scratch, qk_stored, v_stored, units, consts):
    unit0, unit1 = units
    with ExitStack() as ctx:
        def sem(name):
            return ctx.enter_context(nc.semaphore(name))

        w = sbuf(nc, ctx, "w", [P, KD, 3 * D])
        w_hi = sbuf(nc, ctx, "w_hi", [P, KD, 3 * D], F32R)
        w_lo = sbuf(nc, ctx, "w_lo", [P, KD, 3 * D], F32R)
        bqk = sbuf(nc, ctx, "bqk", [P, QKT])
        bv = sbuf(nc, ctx, "bv", [P, D])
        xt = sbuf(nc, ctx, "xt", [P, CT, D])
        xn = sbuf(nc, ctx, "xn", [P, CT, D])
        stats = sbuf(nc, ctx, "stats", [P, CT, 6])
        meanvar = sbuf(nc, ctx, "meanvar", [P, CT, 2])
        var_eps = sbuf(nc, ctx, "var_eps", [P, CT])
        rstd = sbuf(nc, ctx, "rstd", [P, CT])
        xT_hi = sbuf(nc, ctx, "xT_hi", [P, 2, KD, CH], F32R)
        xT_lo = sbuf(nc, ctx, "xT_lo", [P, 2, KD, CH], F32R)
        qk_now = [unit1.q[:, 2 * b:2 * b + 2, :].rearrange("p x (m t) -> p x m t", m=QKT) for b in range(2)]
        qk_hi, qk_lo = [[qk_now[b][:, part] for b in range(2)] for part in range(2)]
        v_room = unit1.v[:].rearrange("p t h w -> p (t h w)")
        vs = [v_room[:, b * CT * D:(b + 1) * CT * D].rearrange("p (g t f) -> p g t f", g=UG, t=CT) for b in range(2)]
        t_ps = banks(nc, ctx, "xT_ps", KD)
        qk_ps = banks(nc, ctx, "qk_ps", QKT)
        v_ps = banks(nc, ctx, "v_ps", VB)

        w_in, b_in, x_in = sem("w_in"), sem("b_in"), sem("x_in")
        ident_set, ident_made, exponent_set = sem("ident_set"), sem("ident_made"), sem("exponent_set")
        w_hi_done, w_lo_done = sem("w_hi_done"), sem("w_lo_done")
        stats_done, aggr_done, rstd_done, normed = sem("stats_done"), sem("aggr_done"), sem("rstd_done"), sem("normed")
        eps_added, passed = sem("eps_added"), sem("passed")
        turned, xT_hi_done, xT_lo_done = sem("turned"), sem("xT_hi_done"), sem("xT_lo_done")
        qk_full, qk_hi_done, qk_lo_done = sem("qk_full"), sem("qk_hi_done"), sem("qk_lo_done")
        v_full, v_done = sem("v_full"), sem("v_done")
        mask_zero, mask_made, rounded = sem("mask_zero"), sem("mask_made"), sem("rounded")
        q_zero, k_ones, v_zero, v_ones = sem("q_zero0"), sem("k_ones0"), sem("v_zero0"), sem("v_ones0")

        block = ctx.enter_context(nc.Block())

        @block.sync
        def _(sp):
            def load_x(n):
                sp.dma_start(xt[:], x[bass.ds(n * CH, CH), :].rearrange("(t p) d -> p t d", p=P)).then_inc(x_in, 16)

            def store(n, b):
                for m in range(QKT):
                    sp.wait_ge(qk_lo_done, n * QKT + (m + 1 + QKT))
                    sp.dma_start(qk_scratch[:, m * P:(m + 1) * P, bass.ds(n * CH, CH)].rearrange("x p t -> p x t"),
                                 qk_now[b][:, :, m, :].bitcast(F32)).then_inc(qk_stored[b][m], 16)
                sp.wait_ge(v_done, n * VB + 2 * VB)
                sp.dma_start(v_scratch[bass.ds(n, 1)].rearrange("a (g p) f -> p (a g) f", p=P),
                             vs[b].rearrange("p g t f -> p g (t f)")).then_inc(v_stored[b], 16)

            for b in range(2):
                for m in range(QKT):
                    sp.sem_inc(qk_stored[b][m], FREE)
                sp.sem_inc(v_stored[b], FREE)
            load_x(0)
            sp.dma_start(w[:], w_exp.rearrange("(k p) n -> p k n", p=P)).then_inc(w_in, 16)
            sp.dma_start(bqk[:], b_exp[0:2 * D].rearrange("(m p) -> p m", p=P),
                         allow_slow_non_contiguous=True).then_inc(b_in, 16)
            sp.dma_start(bv[:], b_exp[2 * D:3 * D].rearrange("(a d) -> a d", a=1).to_broadcast([P, D])).then_inc(b_in, 16)
            for n in range(2):
                sp.wait_ge(normed, (n + 1) * CT)
                load_x(n + 1)
            with sp.Fori(0, QC // 2) as i:
                for b in range(2):
                    sp.wait_ge(normed, (i * 2 + (b + 3)) * CT)
                    load_x(i * 2 + (b + 3))
                    store(i * 2 + b, b)
            sp.wait_ge(normed, (NCH - 1) * CT)
            load_x(NCH - 1)
            for b in range(2):
                for m in range(QKT):
                    sp.wait_ge(qk_stored[b][m], QC // 2 * 16 + FREE)
                sp.wait_ge(v_stored[b], QC // 2 * 16 + FREE)
            sp.wait_ge(q_zero, UH)
            sp.wait_ge(k_ones, 1)
            sp.wait_ge(v_ones, 1)
            for c in range(2):
                store(QC + c, c)
                unit0.load(sp, qk_scratch, v_scratch, 0, c)
            store(QC + 2, 0)
            store(QC + 3, 1)

        @block.gpsimd
        def _(pool):
            pool.memset(consts.ident[:], 0.0).then_inc(ident_set, 1)
            pool.wait_ge(ident_set, 1)
            pool.affine_select(out=consts.ident[:], in_=consts.ident[:], compare_op=ALU.not_equal, fill=1.0, base=0,
                               pattern=[[-1, P]], channel_multiplier=1).then_inc(ident_made, 1)

            def inverse_deviation(n):
                wait_apart(pool, aggr_done, n * CT + CT, passed)
                pool.tensor_scalar(var_eps[:], meanvar[:, :, 1], EPS, None, ALU.add).then_inc(eps_added, 1)
                pool.wait_ge(eps_added, n + 1)
                pool.tensor_tensor(rstd[:], var_eps[:], consts.minus_half[:], ALU.pow).then_inc(rstd_done, 1)

            pool.memset(consts.minus_half[:], -0.5).then_inc(exponent_set, 1)
            pool.wait_ge(exponent_set, 1)
            pool.memset(consts.mask[:], 0.0).then_inc(mask_zero, 1)
            pool.wait_ge(mask_zero, 1)
            pool.affine_select(out=consts.mask[:, CH - P:CH], in_=consts.mask[:, CH - P:CH], compare_op=ALU.is_ge, fill=NEG,
                               base=0, pattern=[[-1, P]], channel_multiplier=1).then_inc(mask_made, 1)
            pool.wait_ge(mask_made, 1)
            for n in range(2):
                inverse_deviation(n)
                for h in range(2 * n, 2 * n + 2):
                    pool.memset(unit0.q[0:ROWS, h].bitcast(F32), 0.0).then_inc(q_zero, 1)
            inverse_deviation(2)
            pool.wait_ge(q_zero, UH)
            pool.wait_ge(rstd_done, 3)
            pool.memset(unit0.k[ROWS:ROWSM].bitcast(F32), 1.0).then_inc(k_ones, 1)
            pool.wait_ge(k_ones, 1)
            pool.memset(unit0.v[:], 0.0).then_inc(v_zero, 1)
            pool.wait_ge(v_zero, 1)
            pool.memset(unit0.v[:, :, :, HD:HD + 1], 1.0).then_inc(v_ones, 1)
            pool.wait_ge(v_ones, 1)
            inverse_deviation(3)
            with pool.Fori(0, NCH - QC) as n:
                inverse_deviation(n + QC)

        @block.scalar
        def _(act):
            def xT_high(n, b):
                for k in range(KD):
                    act.wait_ge(turned, n * KD + k + 1)
                    act.activation(xT_hi[:, b, k, :], t_ps[k][:], ACT.Copy).then_inc(xT_hi_done, 1)

            def qk_high(n, b):
                for m in range(QKT):
                    act.wait_ge(qk_full, n * QKT + m + 1)
                    act.wait_ge(qk_stored[b][m], (n - b) * 8 + FREE)
                    act.activation(qk_hi[b][:, m, :], qk_ps[m][:], ACT.Identity, bias=bqk[:, m:m + 1]
                                   ).then_inc(qk_hi_done, 1)

            act.wait_ge(w_in, 16)
            act.activation(w_hi[:], w[:], ACT.Copy).then_inc(w_hi_done, 1)
            act.wait_ge(b_in, 32)
            xT_high(0, 0)
            with act.Fori(0, NCH // 2 - 1) as i:
                for b in range(2):
                    xT_high(i * 2 + b + 1, 1 - b)
                    qk_high(i * 2 + b, b)
            xT_high(NCH - 1, 1)
            qk_high(NCH - 2, 0)
            qk_high(NCH - 1, 1)

        @block.vector
        def _(dve):
            def norm(n):
                dve.wait_ge(x_in, n * 16 + 16)
                for t in range(CT):
                    dve.bn_stats(stats[:, t, :], xt[:, t, :]).then_inc(stats_done, 1)
                for t in range(CT):
                    wait_apart(dve, stats_done, n * CT + t + 1, passed)
                    dve.bn_aggr(meanvar[:, t, :], stats[:, t, :]).then_inc(aggr_done, 1)
                dve.wait_ge(rstd_done, n + 1)
                for t in range(CT):
                    dve.tensor_scalar(xn[:, t, :], xt[:, t, :], meanvar[:, t, 0:1], rstd[:, t:t + 1],
                                      ALU.subtract, ALU.mult).then_inc(normed, 1)

            def xT_low(n, b):
                for k in range(KD):
                    dve.wait_ge(xT_hi_done, n * KD + k + 1)
                    dve.tensor_tensor(xT_lo[:, b, k, :], t_ps[k][:], xT_hi[:, b, k, :].bitcast(F32), ALU.subtract).then_inc(xT_lo_done, 1)

            def qkv_low(n, b):
                for m in range(QKT):
                    dve.wait_ge(qk_hi_done, n * QKT + m + 1)
                    dve.scalar_tensor_tensor(out=qk_lo[b][:, m, :], in0=qk_ps[m][:], scalar=bqk[:, m:m + 1],
                                             in1=qk_hi[b][:, m, :].bitcast(F32), op0=ALU.add, op1=ALU.subtract).then_inc(qk_lo_done, 1)
                dve.wait_ge(v_stored[b], (n - b) * 8 + FREE)
                for i in range(2):
                    dve.wait_ge(v_full, n * 2 + i + 1)
                    dve.tensor_tensor(vs[b][:, :, 2 * i:2 * i + 2, :].rearrange("p g t f -> p t g f"),
                                      v_ps[i][:].rearrange("p (t g f) -> p t g f", t=2, g=UG),
                                      bv[:, None, :].to_broadcast([P, 2, D]).rearrange("p t (g f) -> p t g f", g=UG),
                                      ALU.add).then_inc(v_done, 1)

            dve.sem_inc(qk_lo_done, QKT)
            dve.sem_inc(v_done, VB)
            norm(0)
            dve.wait_ge(w_hi_done, 1)
            dve.tensor_tensor(w_lo[:], w[:], w_hi[:].bitcast(F32), ALU.subtract).then_inc(w_lo_done, 1)
            dve.wait_ge(b_in, 32)
            xT_low(0, 0)
            norm(1)
            dve.tensor_copy(consts.ident_r[:], consts.ident[:]).then_inc(rounded, 1)
            dve.wait_ge(mask_made, 1)
            dve.tensor_copy(consts.mask_r[:], consts.mask[:, CH - P:CH]).then_inc(rounded, 1)
            with dve.Fori(0, NCH // 2 - 1) as i:
                for b in range(2):
                    xT_low(i * 2 + b + 1, 1 - b)
                    norm(i * 2 + b + 2)
                    qkv_low(i * 2 + b, b)
            xT_low(NCH - 1, 1)
            qkv_low(NCH - 2, 0)
            qkv_low(NCH - 1, 1)

        @block.tensor
        def _(pe):
            def turn(n):
                if not isinstance(n, int) or n > 0:
                    pe.wait_ge(xT_lo_done, n * KD)
                pe.wait_ge(normed, n * CT + CT)
                for k in range(KD):
                    for t in range(CT):
                        mm = pe.transpose(t_ps[k][:, t * P:(t + 1) * P], xn[:, t, k * P:(k + 1) * P], consts.ident[:])
                    mm.then_inc(turned, 1)

            terms = [(w_hi, xT_hi), (w_lo, xT_hi), (w_hi, xT_lo)]

            def project_chunk(n, b):
                pe.wait_ge(xT_lo_done, n * KD + KD)
                for m in range(QKT):
                    pe.wait_ge(qk_lo_done, n * QKT + (m + 1))
                    for i, (k, (wx, xx)) in enumerate([(k, t) for k in range(KD) for t in terms]):
                        mm = pe.matmul(qk_ps[m][:], wx[:, k, m * P:(m + 1) * P], xx[:, b, k, :],
                                       start=(i == 0), stop=(i == 3 * KD - 1))
                    mm.then_inc(qk_full, 1)
                for t in range(CT):
                    if t % 2 == 0:
                        pe.wait_ge(v_done, n * 2 + (t // 2 + 1))
                    for i, (k, (wx, xx)) in enumerate([(k, t_) for k in range(KD) for t_ in terms]):
                        mm = pe.matmul(v_ps[t // 2][:, (t % 2) * D:(t % 2 + 1) * D], xx[:, b, k, t * P:(t + 1) * P],
                                       wx[:, k, 2 * D:3 * D], start=(i == 0), stop=(i == 3 * KD - 1))
                    if t % 2:
                        mm.then_inc(v_full, 1)

            pe.wait_ge(ident_made, 1)
            turn(0)
            pe.wait_ge(w_lo_done, 1)
            with pe.Fori(0, NCH // 2 - 1) as i:
                for b in range(2):
                    turn(i * 2 + b + 1)
                    project_chunk(i * 2 + b, b)
            turn(NCH - 1)
            project_chunk(NCH - 2, 0)
            project_chunk(NCH - 1, 1)


def maxima_events():
    steps = []
    for c in range(QC):
        events = []
        for t in range(CT):
            events += [("scores", c, t, (h,), x) for h in range(UH) for x in range(c)]
            n = {0: UH, 1: 2 if c else 1}.get(t, 1)
            events += [("scores", c, t, tuple(range(h, h + n)), c) for h in range(0, UH, n)]
        at = [len(events) * i // (CT * (c + 1)) for i in range(CT * (c + 1) + 1)]
        steps += [events[lo:hi] for lo, hi in zip(at, at[1:])]
    return steps


def ring_events(first, last):
    maxima = maxima_events()
    steps = []
    for i in range(JU):
        u, a = divmod(i + LEAD, JU)
        now = [] if last and u else [(u, e) for e in maxima[a]]
        for c in range(QC):
            end, start = STEPS_BEFORE[c + 1] + 1, STEPS_BEFORE[c] + 2
            if a == end % JU and not (last and u - end // JU > 0):
                now.append((u - end // JU, ("max_rows", c)))
            if i == start and not (first and c == 0):
                now.append((0 if c else -1, ("ctx_rows", (c - 1) % QC)))
        steps.append(now)
    return steps


def first_events():
    maxima = maxima_events()
    return [[(0, e) for e in maxima[a]] + [(0, ("max_rows", c)) for c in range(QC) if a == STEPS_BEFORE[c + 1] + 1]
            for a in range(LEAD)]


def attend(nc, qk_scratch, v_scratch, qk_stored, v_stored, ctx_scratch, ctx_out, ctx_stored, w_gate, w_up, w_down,
           weights, ops, consts, load_next):
    with ExitStack() as ctx:
        def sem(name):
            return ctx.enter_context(nc.semaphore(name))

        gu_hi, gu_lo, wd_hi, wd_lo = weights
        probs = sbuf(nc, ctx, "probs", [P, PRING, 2, CH])
        part_max = sbuf(nc, ctx, "part_max", [P, 2, UH, CT, QC])
        row_max = sbuf(nc, ctx, "row_max", [P, 2, UH, CT])
        neg_max = sbuf(nc, ctx, "neg_max", [P, 2, UH, 2, CT])
        unread = sbuf(nc, ctx, "unread", [P, RING, CH], BF16)
        max_rows = sbuf(nc, ctx, "max_rows", [2 * UH * CT, 2, P], F32R)
        ctxT = sbuf(nc, ctx, "ctxT", [P, 2, CH])
        inv_sum = sbuf(nc, ctx, "inv_sum", [P, 2, CT * UH])
        ring = banks(nc, ctx, "ring", RING)
        score_ps = [ctx.enter_context(nc.psum_tensor(f"score_ps{p}", [P, 2, CH], F32)) for p in range(PAIRS)]
        out_ps = banks(nc, ctx, "out_ps", 1)[0]

        room = probs[:].rearrange("p n e q -> p (n e q)")
        WN = MF * D
        w_f32 = [room[:, i * WN:(i + 1) * WN] for i in range(3)]
        w_int = [w_f32[i].bitcast(I32) for i in range(3)]
        w_hi, w_lo = [room[:, (3 + i) * WN:(4 + i) * WN] for i in range(2)]
        W_BANKS = WN // CH
        score_banks = [score_ps[q // 2][:, q % 2, :] for q in range(2 * PAIRS)]

        q_zero, k_ones, v_zero, v_ones = sem("q_zero1"), sem("k_ones1"), sem("v_zero1"), sem("v_ones1")
        w_in = [sem(f"w_in{i}") for i in range(3)]
        w_cast, w_rounded, w_rest, w_turned, w_kept = [sem(n) for n in ("w_cast", "w_rounded", "w_rest", "w_turned", "w_kept")]
        ring_full, ring_free, passed = sem("ring_full"), sem("ring_free"), sem("passed1")
        max_done, max_hi_done, max_split = sem("max_done"), sem("max_hi_done"), sem("max_split")
        max_loaded = [sem(f"max_loaded{i}") for i in range(2)]
        scores_full, probs_done, probs_masked = sem("scores_full"), sem("probs_done"), sem("probs_masked")
        pv_done, out_copied, inv_done = sem("pv_done"), sem("out_copied"), sem("inv_done")

        prologue = first_events()
        before_steps = sum(map(len, prologue))
        step_len = sum(map(len, ring_events(False, False)))
        last_events = sum(map(len, ring_events(False, True)))
        assert step_len % RING == 0 and sum(map(len, ring_events(True, False))) == step_len - 1
        NDIAG = CT * PAIRS
        before = STEPS_BEFORE
        ORDER = [(c, jj) for c in range(QC) for jj in range(CT * (c + 1))]
        LAG = 2
        SC, PC = PAIRS, PRING // PAIRS

        def ring_start(s):
            if isinstance(s, int) and s == 0:
                return before_steps
            return s * step_len + (before_steps - 1)

        def slot_base(first):
            return before_steps if first else before_steps - 1

        def in_step(unit, event, s, first=False, last=False):
            return ring_start(s) + ([e for now in ring_events(first, last) for e in now].index((unit, event)) + 1)

        def all_steps(eng, step):
            step(0, 0, True, False)
            with eng.Fori(0, UG - 1) as i:
                step(i, 1, False, False)
                step(i + 1, 0, False, False)
            step(UG - 1, 1, False, True)

        block = ctx.enter_context(nc.Block())

        @block.sync
        def _(sp):
            def place_max(b, c, through):
                sp.wait_ge(ring_free, through)
                for h in range(UH):
                    sp.dma_start(ops[b].q[ROWS:ROWSM, h, c * CH:(c + 1) * CH].bitcast(F32),
                                 max_rows[2 * CT * h:2 * CT * (h + 1), c % 2, :].bitcast(F32)).then_inc(max_loaded[c % 2], 16)

            def store_ctx(i, b, c, through):
                wait_apart(sp, ring_free, through, passed)
                toks = slice(b * S + c * CH, b * S + (c + 1) * CH)
                to = ctx_scratch[toks, bass.ds(i * (UH * HD), UH * HD)].rearrange("(t p) f -> p t f", p=P)
                sp.dma_start(to, ctx_out[:, c % 2].rearrange("p (t h) d -> p t (h d)", h=UH)).then_inc(ctx_stored[c % 2], 16)

            def step(i, b, first, last):
                s = i * 2 + b
                if first:
                    sp.wait_ge(q_zero, 1)
                    sp.wait_ge(k_ones, 1)
                    sp.wait_ge(v_ones, 1)
                elif not last:
                    wait_apart(sp, pv_done, s * JU + PC, passed)
                chunk = 0
                for unit, event in (e for now in ring_events(first, last) for e in now):
                    kind, c = event[0], event[1]
                    if kind == "max_rows":
                        place_max(b ^ unit, c, in_step(unit, event, s, first, last))
                    if kind == "ctx_rows":
                        store_ctx(i + (b - 1 if unit else 0), b ^ -unit, c, in_step(unit, event, s, first, last))
                    if kind != "scores" and chunk < QC and not last:
                        ops[1 - b].load(sp, qk_scratch, v_scratch, i + b, chunk)
                        chunk += 1

            sp.dma_start(w_int[0].rearrange("p (m d) -> p m d", m=MF), w_gate.rearrange("(m p) d -> p m d", p=P)).then_inc(w_in[0], 16)
            sp.dma_start(w_int[1].rearrange("p (m d) -> p m d", m=MF), w_up.rearrange("(m p) d -> p m d", p=P)).then_inc(w_in[1], 16)
            sp.dma_start(w_int[2].rearrange("p (k f) -> p k f", k=KD), w_down.rearrange("(k p) f -> p k f", p=P)).then_inc(w_in[2], 16)
            for c in range(2, QC):
                ops[0].load(sp, qk_scratch, v_scratch, 0, c)
            flat = [e for now in prologue for e in now]
            for k, (unit, event) in enumerate(flat):
                if event[0] == "max_rows":
                    place_max(0, event[1], k + 1)
            for stored in qk_stored[0] + qk_stored[1] + v_stored:
                sp.wait_ge(stored, NCH // 2 * 16 + FREE)
            all_steps(sp, step)
            for i in range(2):
                sp.wait_ge(ctx_stored[i], 16 * sum(c % 2 == i for c in range(B * UG * QC - 1)))
            load_next(sp)
            store_ctx(UG - 1, 1, QC - 1, ring_start(2 * UG - 1) + last_events + 1)

        @block.gpsimd
        def _(pool):
            for w in range(3):
                pool.wait_ge(w_cast, w + 1)
                if w:
                    pool.wait_ge(w_turned, 2 * W_BANKS * w)
                pool.tensor_tensor(w_lo, w_f32[w], w_hi, ALU.subtract).then_inc(w_rest, 1)
            pool.wait_ge(w_rest, 3)
            for stored in qk_stored[0] + qk_stored[1] + v_stored:
                pool.wait_ge(stored, NCH // 2 * 16 + FREE)
            pool.memset(ops[1].q[0:ROWS].bitcast(F32), 0.0).then_inc(q_zero, 1)
            pool.wait_ge(q_zero, 1)
            pool.memset(ops[1].k[ROWS:ROWSM].bitcast(F32), 1.0).then_inc(k_ones, 1)
            pool.wait_ge(k_ones, 1)
            pool.memset(ops[1].v[:], 0.0).then_inc(v_zero, 1)
            pool.wait_ge(v_zero, 1)
            pool.memset(ops[1].v[:, :, :, HD:HD + 1], 1.0).then_inc(v_ones, 1)
            pool.wait_ge(v_ones, 1)

            def step(i, b, first, last):
                s = i * 2 + b
                for c in range(QC):
                    for r in range(CT):
                        j = before[c] + CT * c + r
                        for pair in range(PAIRS):
                            n = PAIRS * j + pair
                            wait_apart(pool, probs_done, s * (PAIRS * JU) + (n + 1 + SC), passed)
                            at = probs[:, n % PRING, :, P * r:P * (r + 1)]
                            pool.affine_select(out=at, in_=at, compare_op=ALU.is_ge, fill=0.0, base=0,
                                               pattern=[[0, 2], [1, P]], channel_multiplier=-1).then_inc(probs_masked, 1)

            all_steps(pool, step)

        @block.scalar
        def _(act):
            act.sem_inc(probs_done, SC)
            act.sem_inc(out_copied, FREE)
            for w in range(3):
                act.wait_ge(w_in[w], 16)
                if w:
                    act.wait_ge(w_rest, w)
                    act.wait_ge(w_turned, 2 * W_BANKS * w - W_BANKS)
                act.activation(w_hi.bitcast(F32R), w_int[w], ACT.Copy).then_inc(w_rounded, 1)
                act.wait_ge(w_rounded, w + 1)
                act.activation(w_f32[w], w_int[w], ACT.Copy).then_inc(w_cast, 1)
                for part, to in enumerate([(gu_hi, gu_lo), (gu_hi, gu_lo), (wd_hi, wd_lo)][w]):
                    to = to[:, w].rearrange("p k f -> p (k f)") if w < 2 else to[:].rearrange("p m d -> p (m d)")
                    for r in range(W_BANKS):
                        q = (2 * w + part) * W_BANKS + r
                        act.wait_ge(w_turned, q + 1)
                        act.activation(to[:, r * CH:(r + 1) * CH], score_banks[q % 4], ACT.Copy).then_inc(w_kept, 1)

            def copy_out(u, c):
                act.wait_ge(pv_done, u * JU + (before[c + 1] + PC))
                if not (isinstance(u, int) and u * QC + c < 2):
                    act.wait_ge(inv_done, u * QC + (c - 1))
                act.activation(ctxT[:, c % 2, :], out_ps[:], ACT.Copy).then_inc(out_copied, 1)

            def step(i, b, first, last):
                s = i * 2 + b
                for c, jj in ORDER:
                    j = before[c] + jj
                    lo = P * max(0, jj - CT * c)
                    for pair in range(PAIRS):
                        n = PAIRS * j + pair
                        act.wait_ge(scores_full, s * (PAIRS * JU) + (n + 1))
                        if pair == 0:
                            act.wait_ge(pv_done, s * JU + (j + 1))
                        act.activation(probs[:, n % PRING, :, lo:CH], score_ps[pair][:, :, lo:CH], ACT.Exp,
                                       scale=SCALE).then_inc(probs_done, 1)
                    if jj == LAG - 1 and not (first and c == 0):
                        copy_out(*((s, c - 1) if c else (s - 1, QC - 1)))

            act.wait_ge(w_turned, 6 * W_BANKS)
            all_steps(act, step)
            copy_out(2 * UG - 1, QC - 1)

        @block.vector
        def _(dve):
            def take(u, event, k, start):
                kind, c = event[0], event[1]
                bank = ring[k % RING]
                masked = kind == "scores" and event[4] == c and len(event[3]) == 1
                if masked:
                    wait_apart(dve, ring_full, start + 1, passed)
                else:
                    dve.wait_ge(ring_full, start + 1)
                if kind == "scores":
                    _, _, t, heads, x = event
                    n = P * (t + 1) if x == c else CH
                    if masked:
                        dve.tensor_tensor_reduce(unread[:, k % RING, 0:n], bank[:, 0:n], consts.mask[:, CH - n:CH], 1.0, NEG,
                                                 ALU.add, ALU.max, part_max[:, c % 2, heads[0], t, x:x + 1]
                                                 ).then_inc(ring_free, 1)
                    else:
                        dve.tensor_reduce(part_max[:, c % 2, heads[0]:heads[-1] + 1, t, x],
                                          bank[:, 0:len(heads) * n].rearrange("p (h q) -> p h q", q=n), AX.X, ALU.max
                                          ).then_inc(ring_free, 1)
                    if (t, heads[-1], x) == (CT - 1, UH - 1, c):
                        m = u * QC + c
                        dve.wait_ge(ring_free, start + 1)
                        dve.tensor_reduce(row_max[:, c % 2].rearrange("p h t -> p (h t)"), part_max[:, c % 2].rearrange("p h t x -> p (h t) x")[:, :, 0:c + 1], AX.X, ALU.max
                                          ).then_inc(max_done, 1)
                        dve.wait_ge(max_done, m + 1)
                        dve.tensor_scalar(neg_max[:, c % 2, :, 0, :].bitcast(F32R), row_max[:, c % 2], -1.0, None, ALU.mult
                                          ).then_inc(max_hi_done, 1)
                        dve.wait_ge(max_hi_done, m + 1)
                        dve.scalar_tensor_tensor(out=neg_max[:, c % 2, :, 1, :], in0=row_max[:, c % 2], scalar=-1.0,
                                                 in1=neg_max[:, c % 2, :, 0, :], op0=ALU.mult, op1=ALU.subtract
                                                 ).then_inc(max_split, 1)
                elif kind == "max_rows":
                    if not (isinstance(u, int) and u * QC + c < 2):
                        dve.wait_ge(max_loaded[c % 2], u * 128 + 64 * (c // 2))
                    dve.tensor_copy(max_rows[:, c % 2, :], bank[0:2 * UH * CT, 0:P]).then_inc(ring_free, 1)
                else:
                    rows = bank[:].rearrange("p (n w) -> p n w", w=VW)
                    dve.reciprocal(inv_sum[:, c % 2], rows[:, :, HD]).then_inc(inv_done, 1)
                    if not (isinstance(u, int) and u * QC + c < 2):
                        dve.wait_ge(ctx_stored[c % 2], u * 32 + 16 * (c // 2))
                    dve.wait_ge(inv_done, u * QC + (c + 1))
                    dve.tensor_tensor(ctx_out[:, c % 2], rows[:, :, 0:HD],
                                      inv_sum[:, c % 2, :, None].to_broadcast([P, CT * UH, HD]), ALU.mult).then_inc(ring_free, 1)

            for k, (unit, event) in enumerate(e for now in prologue for e in now):
                take(unit, event, k, k)

            def step(i, b, first, last):
                s = i * 2 + b
                for k, (unit, event) in enumerate(e for now in ring_events(first, last) for e in now):
                    take(s + unit, event, slot_base(first) + k, ring_start(s) + k)

            all_steps(dve, step)
            take(2 * UG - 1, ("ctx_rows", QC - 1), slot_base(False) + last_events, ring_start(2 * UG - 1) + last_events)

        @block.tensor
        def _(pe):
            pe.sem_inc(pv_done, PC)

            def fill(u, b, event, k, start):
                kind, c = event[0], event[1]
                bank = ring[k % RING]
                if not (isinstance(start, int) and start < RING):
                    pe.wait_ge(ring_free, start - (RING - 1))
                if kind == "scores":
                    _, _, t, heads, x = event
                    q, keys = ops[b].q, ops[b].k
                    q_at = c * CH + t * P
                    n = P * (t + 1) if x == c else CH
                    for e, h in enumerate(heads):
                        mm = pe.matmul(bank[:, e * n:(e + 1) * n], q[0:ROWS, h, q_at:q_at + P],
                                       keys[0:ROWS, h // 2, x * CH:x * CH + n], start=(e == 0), stop=True,
                                       skip_group_check=True)
                    if x == c and len(heads) > 1:
                        last_keys = bank[:, 0:len(heads) * n].rearrange("p (h k) -> p h k", k=n)[:, :, n - P:n]
                        mm = pe.matmul(last_keys, consts.ident_r[:], consts.mask_r[:, None, :].to_broadcast([P, len(heads), P]),
                                       start=False, stop=True, skip_group_check=True)
                elif kind == "max_rows":
                    pe.wait_ge(max_split, u * QC + (c + 1))
                    mm = pe.transpose(bank[0:2 * UH * CT, 0:P], neg_max[:, c % 2].rearrange("p h x t -> p (h x t)"), consts.ident[:])
                else:
                    pe.wait_ge(out_copied, u * QC + (c + 1 + FREE))
                    for t in range(CT):
                        mm = pe.transpose(bank[:, t * P:(t + 1) * P], ctxT[:, c % 2, t * P:(t + 1) * P], consts.ident[:])
                mm.then_inc(ring_full, 1)

            def scores(s, b, c, jj, pair):
                n = PAIRS * (before[c] + jj) + pair
                lo = P * max(0, jj - CT * c)
                pe.wait_ge(probs_done, s * (PAIRS * JU) + (n - PAIRS + 1 + SC))
                for e in range(2):
                    mm = pe.matmul(score_ps[pair][:, e, lo:CH], ops[b].k[0:ROWSM, pair, jj * P:(jj + 1) * P],
                                   ops[b].q[0:ROWSM, 2 * pair + e, c * CH + lo:(c + 1) * CH], start=True, stop=True)
                mm.then_inc(scores_full, 1)

            def weigh(u, b, c, jj):
                j = before[c] + jj
                diag = jj - CT * c
                lo = P * max(0, diag)
                if diag == 0:
                    pe.wait_ge(ops[b].v_loaded[c], loads_of(u, b, V_LOADS))
                if jj == 0:
                    pe.wait_ge(out_copied, u * QC + (c + FREE))
                if diag >= 0:
                    pe.wait_ge(probs_masked, u * (QC * NDIAG) + (NDIAG * c + PAIRS * (diag + 1)))
                else:
                    pe.wait_ge(probs_done, u * (PAIRS * JU) + (PAIRS * (j + 1) + SC))
                for h in range(UH):
                    mm = pe.matmul(out_ps[VW * h:VW * (h + 1), lo:CH], ops[b].v[:, jj, h, :],
                                   probs[:, (PAIRS * j + h // 2) % PRING, h % 2, lo:CH],
                                   start=(jj == 0), stop=(jj == CT * (c + 1) - 1), skip_group_check=True)
                mm.then_inc(pv_done, 1)

            def loads_of(u, b, dmas):
                return u * (dmas // 2) + (dmas // 2) * (2 - b)

            def turn_weights(q):
                w, part, r = q // (2 * W_BANKS), q // W_BANKS % 2, q % W_BANKS
                if r == 0:
                    pe.wait_ge(w_rest if part else w_rounded, w + 1)
                if q >= len(score_banks):
                    pe.wait_ge(w_kept, q - len(score_banks) + 1)
                for a in range(CT):
                    block_ = r * CT + a
                    at = (block_ % MF) * D + (block_ // MF) * P if w < 2 else (block_ % KD) * FH + (block_ // KD) * P
                    mm = pe.transpose(score_banks[q % 4][:, a * P:(a + 1) * P], (w_lo if part else w_hi)[:, at:at + P], consts.ident[:])
                mm.then_inc(w_turned, 1)

            k = q = 0
            for (c, jj), now in zip(ORDER, prologue):
                if jj == 0:
                    pe.wait_ge(ops[0].loaded[c], QK_LOADS)
                for unit, event in now:
                    fill(0, 0, event, k, k)
                    k += 1
                    while q < 6 * W_BANKS and k >= W_FIRST + (before_steps - W_FIRST) * q // (6 * W_BANKS):
                        turn_weights(q)
                        q += 1
            pe.wait_ge(w_kept, 6 * W_BANKS)

            def step(i, b, first, last):
                s = i * 2 + b
                pending = [] if first else [(s - 1, 1 - b, *ORDER[a - LAG]) for a in range(LAG)]
                k = 0

                def fills(events):
                    nonlocal k
                    for unit, event in events:
                        fill(s + unit, b ^ (unit == 1), event, slot_base(first) + k, ring_start(s) + k)
                        k += 1

                for j, ((c, jj), now) in enumerate(zip(ORDER, ring_events(first, last))):
                    ahead, a = divmod(j + LEAD, JU)
                    if ORDER[a][1] == 0 and not (last and ahead):
                        buffer = b ^ ahead
                        pe.wait_ge(ops[buffer].loaded[ORDER[a][0]], loads_of(s + ahead, buffer, QK_LOADS))
                    if jj == 0:
                        pe.wait_ge(max_loaded[c % 2], s * 128 + 64 * (c // 2 + 1))
                    pending.append((s, b, c, jj))
                    scores(s, b, c, jj, 0)
                    fills(now[0:1])
                    scores(s, b, c, jj, 1)
                    fills(now[1:3])
                    if len(pending) > LAG:
                        weigh(*pending.pop(0))
                    fills(now[3:])

            all_steps(pe, step)
            for a in range(LAG):
                weigh(2 * UG - 1, 1, *ORDER[a - LAG])
            fill(2 * UG - 1, 1, ("ctx_rows", QC - 1), slot_base(False) + last_events, ring_start(2 * UG - 1) + last_events)


class Constants:

    def __init__(self, nc, ctx):
        self.ident = sbuf(nc, ctx, "ident", [P, P])
        self.ident_r = sbuf(nc, ctx, "ident_r", [P, P], F32R)
        self.mask = sbuf(nc, ctx, "mask", [P, CH])
        self.mask_r = sbuf(nc, ctx, "mask_r", [P, P], F32R)
        self.minus_half = sbuf(nc, ctx, "minus_half", [P, CT])


class FirstLoads:

    def __init__(self, nc, ctx, w_comp, b_comp, ctx_scratch):
        self.wc = sbuf(nc, ctx, "wc", [P, KD, D])
        self.bc = sbuf(nc, ctx, "bc", [P, D])
        self.ctx_now = sbuf(nc, ctx, "ctx_now", [P, CT, D])
        self.wc_in, self.bc_in, self.ctx_in = [
            ctx.enter_context(nc.semaphore(name)) for name in ("wc_in", "bc_in", "ctx_in")]
        self.w_comp, self.b_comp, self.ctx_scratch = w_comp, b_comp, ctx_scratch

    def load_ctx(self, sp, n):
        sp.dma_start(self.ctx_now[:], self.ctx_scratch[bass.ds(n * CH, CH), :].rearrange("(t p) d -> p t d", p=P)
                     ).then_inc(self.ctx_in, 16)

    def start(self, sp):
        sp.dma_start(self.wc[:], self.w_comp.rearrange("(k p) n -> p k n", p=P)).then_inc(self.wc_in, 16)
        self.load_ctx(sp, 0)
        sp.dma_start(self.bc[:], self.b_comp.rearrange("(a d) -> a d", a=1).to_broadcast([P, D])).then_inc(self.bc_in, 16)


def feed(nc, x, first, out, ctx_stored, weights, consts):
    with ExitStack() as ctx:
        def sem(name):
            return ctx.enter_context(nc.semaphore(name))

        wc, bc, ctx_now = first.wc, first.bc, first.ctx_now
        wc_in, bc_in, ctx_in, x_in = first.wc_in, first.bc_in, first.ctx_in, sem("x2_in")
        xr = sbuf(nc, ctx, "xr", [P, CT, D])
        gu_hi, gu_lo, wd_hi, wd_lo = weights
        wc_hi = sbuf(nc, ctx, "wc_hi", [P, KD, D], F32R)
        wc_lo = sbuf(nc, ctx, "wc_lo", [P, KD, D], F32R)
        xb = sbuf(nc, ctx, "xb", [P, CT, D])
        cT_hi = sbuf(nc, ctx, "cT_hi", [P, KD, CH], F32R)
        cT_lo = sbuf(nc, ctx, "cT_lo", [P, KD, CH], F32R)
        x1 = sbuf(nc, ctx, "x1", [P, CT, D])
        x1_kept = sbuf(nc, ctx, "x1_kept", [P, CT, D])
        stats = sbuf(nc, ctx, "stats2", [P, CT, 6])
        meanvar = sbuf(nc, ctx, "meanvar2", [P, CT, 2])
        var_eps = sbuf(nc, ctx, "var_eps2", [P, CT])
        rstd = sbuf(nc, ctx, "rstd2", [P, CT])
        xn = sbuf(nc, ctx, "xn2", [P, CT, D])
        xT_hi = sbuf(nc, ctx, "x2T_hi", [P, KD, CH], F32R)
        xT_lo = sbuf(nc, ctx, "x2T_lo", [P, KD, CH], F32R)
        silu = sbuf(nc, ctx, "silu", [P, 2, CH])
        h = sbuf(nc, ctx, "h", [P, HB, CH])
        h_hi = sbuf(nc, ctx, "h_hi", [P, MF, CH], F32R)
        h_lo = sbuf(nc, ctx, "h_lo", [P, MF, CH], F32R)
        res = sbuf(nc, ctx, "res", [P, CT, D])
        t_ps = banks(nc, ctx, "turn_ps", 2)
        y_ps = banks(nc, ctx, "y_ps", 2)
        g_ps = banks(nc, ctx, "g_ps", 2)
        u_ps = banks(nc, ctx, "u_ps", 2)

        wc_hi_done, wc_lo_done = sem("wc_hi_done"), sem("wc_lo_done")
        xb_done, x1_moved = sem("xb_done"), sem("x1_moved")
        turned, hi_done, lo_done = sem("turned2"), sem("hi_done"), sem("lo_done")
        y_full, x1_done = sem("y_full"), sem("x1_done")
        stats_done, aggr_done, rstd_done, normed = sem("stats2_done"), sem("aggr2_done"), sem("rstd2_done"), sem("normed2")
        eps_added, passed = sem("eps2_added"), sem("passed2")
        gu_full, silu_done, h_done = sem("gu_full"), sem("silu_done"), sem("h_done")
        h_hi_done, h_lo_done = sem("h_hi_done"), sem("h_lo_done")
        down_full, res_done, stored = sem("down_full"), sem("res_done"), sem("stored")

        block = ctx.enter_context(nc.Block())

        @block.sync
        def _(sp):
            def store(n):
                sp.wait_ge(res_done, n * 2 + 2)
                sp.dma_start(out[bass.ds(n * CH, CH), :].rearrange("(t p) d -> p t d", p=P), res[:]).then_inc(stored, 16)

            def load_x(n):
                sp.dma_start(xr[:], x[bass.ds(n * CH, CH), :].rearrange("(t p) d -> p t d", p=P)).then_inc(x_in, 16)

            def load(n):
                sp.wait_ge(turned, n * (2 * KD) - KD)
                first.load_ctx(sp, n)
                sp.wait_ge(xb_done, n)
                load_x(n)

            sp.sem_inc(stored, FREE)
            load_x(0)
            load(1)
            with sp.Fori(0, QC - 2) as n:
                load(n + 2)
                store(n)
            for i in range(2):
                sp.wait_ge(ctx_stored[i], B * UG * QC * 8)
            with sp.Fori(QC - 2, NCH - 2) as n:
                load(n + 2)
                store(n)
            store(NCH - 2)
            store(NCH - 1)
            sp.wait_ge(stored, NCH * 16 + FREE)

        @block.gpsimd
        def _(pool):
            def inverse_deviation(n):
                wait_apart(pool, aggr_done, n * CT + CT, passed)
                pool.tensor_scalar(var_eps[:], meanvar[:, :, 1], EPS, None, ALU.add).then_inc(eps_added, 1)
                pool.wait_ge(eps_added, n + 1)
                pool.tensor_tensor(rstd[:], var_eps[:], consts.minus_half[:], ALU.pow).then_inc(rstd_done, 1)

            def add_bias(n):
                pool.wait_ge(x_in, n * 16 + 16)
                if not isinstance(n, int) or n > 0:
                    pool.wait_ge(x1_done, n * 2)
                pool.tensor_tensor(xb[:], xr[:], bc[:, None, :].to_broadcast([P, CT, D]), ALU.add).then_inc(xb_done, 1)

            def keep(n):
                pool.wait_ge(x1_done, n * 2 + 2)
                if not isinstance(n, int) or n > 0:
                    wait_apart(pool, res_done, n * 2, passed)
                pool.tensor_copy(x1_kept[:], x1[:]).then_inc(x1_moved, 1)

            pool.wait_ge(bc_in, 16)
            add_bias(0)
            inverse_deviation(0)
            add_bias(1)
            keep(0)
            with pool.Fori(0, NCH - 2) as n:
                inverse_deviation(n + 1)
                add_bias(n + 2)
                keep(n + 1)
            inverse_deviation(NCH - 1)
            keep(NCH - 1)

        @block.scalar
        def _(act):
            def high(n, which, to):
                for k in range(KD):
                    act.wait_ge(turned, n * (2 * KD) + (which * KD + k + 1))
                    act.activation(to[:, k, :], t_ps[k][:], ACT.Copy).then_inc(hi_done, 1)

            def gate(n, m):
                act.wait_ge(gu_full, n * MF + (m + 1))
                act.activation(silu[:, m % 2, :], g_ps[m % 2][:], ACT.Silu, scale=W_SCALE).then_inc(silu_done, 1)

            def hidden_high(n, m):
                act.wait_ge(h_done, n * MF + (m + 1))
                act.activation(h_hi[:, m, :], h[:, m % HB, :], ACT.Copy).then_inc(h_hi_done, 1)

            act.wait_ge(wc_in, 16)
            act.activation(wc_hi[:], wc[:], ACT.Copy).then_inc(wc_hi_done, 1)
            high(0, 0, cT_hi)
            high(0, 1, xT_hi)
            with act.Fori(0, NCH - 1) as n:
                gate(n, 0)
                high(n + 1, 0, cT_hi)
                for m in range(1, MF):
                    hidden_high(n, m - 1)
                    gate(n, m)
                hidden_high(n, MF - 1)
                high(n + 1, 1, xT_hi)
            gate(NCH - 1, 0)
            for m in range(1, MF):
                hidden_high(NCH - 1, m - 1)
                gate(NCH - 1, m)
            hidden_high(NCH - 1, MF - 1)

        @block.vector
        def _(dve):
            def low(n, which, to, hi):
                for k in range(KD):
                    dve.wait_ge(hi_done, n * (2 * KD) + (which * KD + k + 1))
                    dve.tensor_tensor(to[:, k, :], t_ps[k][:], hi[:, k, :].bitcast(F32), ALU.subtract).then_inc(lo_done, 1)

            def residual(n):
                dve.wait_ge(xb_done, n + 1)
                if not isinstance(n, int) or n > 0:
                    dve.wait_ge(x1_moved, n)
                for i in range(2):
                    dve.wait_ge(y_full, n * 2 + i + 1)
                    dve.tensor_tensor(x1[:, 2 * i:2 * i + 2, :], y_ps[i][:].rearrange("p (t d) -> p t d", d=D),
                                      xb[:, 2 * i:2 * i + 2, :], ALU.add).then_inc(x1_done, 1)

            def statistics(n):
                dve.wait_ge(x1_done, n * 2 + 2)
                for t in range(CT):
                    dve.bn_stats(stats[:, t, :], x1[:, t, :]).then_inc(stats_done, 1)
                for t in range(CT):
                    wait_apart(dve, stats_done, n * CT + t + 1, passed)
                    dve.bn_aggr(meanvar[:, t, :], stats[:, t, :]).then_inc(aggr_done, 1)

            def norm(n):
                dve.wait_ge(rstd_done, n + 1)
                for t in range(CT):
                    dve.tensor_scalar(xn[:, t, :], x1[:, t, :], meanvar[:, t, 0:1], rstd[:, t:t + 1],
                                      ALU.subtract, ALU.mult).then_inc(normed, 1)

            def hidden(n, m):
                dve.wait_ge(h_lo_done, n * MF + (m + 1))
                dve.wait_ge(silu_done, n * MF + (m + 1))
                dve.scalar_tensor_tensor(out=h[:, m % HB, :], in0=u_ps[m % 2][:], scalar=W_SCALE, in1=silu[:, m % 2, :],
                                         op0=ALU.mult, op1=ALU.mult).then_inc(h_done, 1)

            def hidden_low(n, m):
                dve.wait_ge(h_hi_done, n * MF + (m + 1))
                dve.tensor_tensor(h_lo[:, m, :], h[:, m % HB, :], h_hi[:, m, :].bitcast(F32), ALU.subtract).then_inc(h_lo_done, 1)

            def result(n):
                dve.wait_ge(x1_moved, n + 1)
                dve.wait_ge(stored, n * 16 + FREE)
                for i in range(2):
                    dve.wait_ge(down_full, n * 2 + i + 1)
                    dve.scalar_tensor_tensor(out=res[:, 2 * i:2 * i + 2, :], in0=y_ps[i][:].rearrange("p (t d) -> p t d", d=D),
                                             scalar=W_SCALE, in1=x1_kept[:, 2 * i:2 * i + 2, :],
                                             op0=ALU.mult, op1=ALU.add).then_inc(res_done, 1)

            dve.sem_inc(h_lo_done, HB)
            dve.wait_ge(wc_hi_done, 1)
            dve.tensor_tensor(wc_lo[:], wc[:], wc_hi[:].bitcast(F32), ALU.subtract).then_inc(wc_lo_done, 1)
            low(0, 0, cT_lo, cT_hi)
            residual(0)
            statistics(0)
            norm(0)
            low(0, 1, xT_lo, xT_hi)
            with dve.Fori(0, NCH - 1) as n:
                hidden(n, 0)
                low(n + 1, 0, cT_lo, cT_hi)
                hidden_low(n, 0)
                hidden(n, 1)
                hidden_low(n, 1)
                hidden(n, 2)
                residual(n + 1)
                statistics(n + 1)
                hidden_low(n, 2)
                hidden(n, 3)
                norm(n + 1)
                for m in range(4, MF):
                    hidden_low(n, m - 1)
                    hidden(n, m)
                hidden_low(n, MF - 1)
                low(n + 1, 1, xT_lo, xT_hi)
                result(n)
            hidden(NCH - 1, 0)
            for m in range(1, MF):
                hidden_low(NCH - 1, m - 1)
                hidden(NCH - 1, m)
            hidden_low(NCH - 1, MF - 1)
            result(NCH - 1)

        @block.tensor
        def _(pe):
            def turn(n, which, src, ready, count):
                pe.wait_ge(ready, count)
                for k in range(KD):
                    for t in range(CT):
                        mm = pe.transpose(t_ps[k][:, t * P:(t + 1) * P], src[:, t, k * P:(k + 1) * P], consts.ident[:])
                    mm.then_inc(turned, 1)

            def out_project(n):
                pe.wait_ge(lo_done, n * (2 * KD) + KD)
                terms = [(cT_hi, wc_hi), (cT_lo, wc_hi), (cT_hi, wc_lo)]
                for t in range(CT):
                    for i, (k, (cx, wx)) in enumerate([(k, t_) for k in range(KD) for t_ in terms]):
                        mm = pe.matmul(y_ps[t // 2][:, (t % 2) * D:(t % 2 + 1) * D], cx[:, k, t * P:(t + 1) * P],
                                       wx[:, k, :], start=(i == 0), stop=(i == 3 * KD - 1))
                    if t % 2:
                        mm.then_inc(y_full, 1)

            def gate_up(n, m):
                if m == 0:
                    pe.wait_ge(lo_done, n * (2 * KD) + 2 * KD)
                if m >= 2:
                    pe.wait_ge(h_done, n * MF + (m - 1))
                terms = [(gu_hi, xT_hi), (gu_lo, xT_hi), (gu_hi, xT_lo)]
                for which, bank in ((0, g_ps[m % 2]), (1, u_ps[m % 2])):
                    for i, (k, (wx, xx)) in enumerate([(k, t_) for k in range(KD) for t_ in terms]):
                        mm = pe.matmul(bank[:], wx[:, which, k, m * P:(m + 1) * P], xx[:, k, :],
                                       start=(i == 0), stop=(i == 3 * KD - 1))
                mm.then_inc(gu_full, 1)

            def down(n):
                pe.wait_ge(h_lo_done, n * MF + (MF - 1 + HB))
                terms = [(h_hi, wd_hi), (h_lo, wd_hi), (h_hi, wd_lo)]
                for t in range(CT):
                    for i, (m, (hx, wx)) in enumerate([(m, t_) for m in range(MF) for t_ in terms]):
                        if t == 0 and i == 3 * (MF - 1):
                            pe.wait_ge(h_lo_done, n * MF + (MF + HB))
                        mm = pe.matmul(y_ps[t // 2][:, (t % 2) * D:(t % 2 + 1) * D], hx[:, m, t * P:(t + 1) * P],
                                       wx[:, m, :], start=(i == 0), stop=(i == 3 * MF - 1))
                    if t % 2:
                        mm.then_inc(down_full, 1)

            turn(0, 0, ctx_now, ctx_in, 16)
            pe.wait_ge(wc_lo_done, 1)
            out_project(0)
            turn(0, 1, xn, normed, CT)
            with pe.Fori(0, NCH - 1) as n:
                gate_up(n, 0)
                turn(n + 1, 0, ctx_now, ctx_in, n * 16 + 32)
                gate_up(n, 1)
                gate_up(n, 2)
                out_project(n + 1)
                for m in range(3, MF):
                    gate_up(n, m)
                turn(n + 1, 1, xn, normed, n * CT + 2 * CT)
                down(n)
            for m in range(MF):
                gate_up(NCH - 1, m)
            down(NCH - 1)


def layer(nc, x, w_exp, b_exp, w_comp, b_comp, w_gate, w_up, w_down, out):
    qk_scratch = nc.dram_tensor("qk_scratch", [2, 2 * D, TOK], F32, kind="Internal").ap()
    v_scratch = nc.dram_tensor("v_scratch", [NCH, UG * P, CT * UH * HD], F32, kind="Internal").ap()
    ctx_scratch = nc.dram_tensor("ctx_scratch", [TOK, D], F32, kind="Internal").ap()
    x2d = x.rearrange("b s d -> (b s) d")
    out2d = out.rearrange("b s d -> (b s) d")
    with ExitStack() as ctx:
        consts = Constants(nc, ctx)
        weights = (sbuf(nc, ctx, "gu_hi", [P, 2, KD, FH], F32R), sbuf(nc, ctx, "gu_lo", [P, 2, KD, FH], F32R),
                   sbuf(nc, ctx, "wd_hi", [P, MF, D], F32R), sbuf(nc, ctx, "wd_lo", [P, MF, D], F32R))
        first = FirstLoads(nc, ctx, w_comp, b_comp, ctx_scratch)
        ctx_out = sbuf(nc, ctx, "ctx_out", [P, 2, CT * UH, HD])
        ctx_stored = [ctx.enter_context(nc.semaphore(f"ctx_stored{i}")) for i in range(2)]
        with ExitStack() as inner:
            units = [Operands(nc, inner, b) for b in range(B)]
            qk_stored = [[inner.enter_context(nc.semaphore(f"qk_stored{b}_{m}")) for m in range(QKT)] for b in range(2)]
            v_stored = [inner.enter_context(nc.semaphore(f"v_stored{b}")) for b in range(2)]
            project(nc, x2d, w_exp, b_exp, qk_scratch, v_scratch, qk_stored, v_stored, units, consts)
            attend(nc, qk_scratch, v_scratch, qk_stored, v_stored, ctx_scratch, ctx_out, ctx_stored,
                   w_gate, w_up, w_down, weights, units, consts, first.start)
        feed(nc, x2d, first, out2d, ctx_stored, weights, consts)


_INS = ["L0_attn_x", "L0_attn_W_exp", "L0_attn_b_exp", "L0_attn_W_comp", "L0_attn_b_comp",
        "L0_ffn_w_gate", "L0_ffn_w_up", "L0_ffn_w_down"]


def kernel(**inputs):
    import numpy as np
    import concourse.bacc as bacc
    from concourse.bass_utils import run_bass_kernel_spmd

    nc = bacc.Bacc("TRN2", target_bir_lowering=False, num_devices=1)
    arrays, args = {}, []
    for name in _INS:
        a = np.ascontiguousarray(inputs[name])
        arrays[f"in_{name}"] = a
        args.append(nc.dram_tensor(f"in_{name}", a.shape, mybir.dt.from_np(a.dtype), kind="ExternalInput").ap())
    args.append(nc.dram_tensor("out_x", (B, S, D), F32, kind="ExternalOutput").ap())
    layer(nc, *args)
    r = run_bass_kernel_spmd(nc, [arrays], core_ids=[0])
    return r.results[0]["out_x"]
```
